# Optimizing a Trainium2 kernel written in Bass

```python
import numpy as np
import jax
import jax.numpy as jnp

def _softmax(x, axis=-1):
    return jax.nn.softmax(x, axis=axis)

def _gelu(x):
    return jax.nn.gelu(x, approximate=True)

def _silu(x):
    return jax.nn.silu(x)

def _sigmoid(x):
    return jax.nn.sigmoid(x)

def _layernorm(x, axis=-1, eps=1e-05):
    m = jnp.mean(x, axis=axis, keepdims=True)
    v = jnp.var(x, axis=axis, keepdims=True)
    return (x - m) / jnp.sqrt(v + eps)

def _scatter_add(tgt, idx, src, axis=0):
    return tgt.at[idx].add(src)

def _segment_sum(src, seg, n):
    return jax.ops.segment_sum(src, seg, n)
kernel_name = 'mk_adj_preln_d2_adj_r2_1492f6'

def setup_inputs(seed: int=0):
    np.random.seed(seed)
    _w = jnp.asarray

    def _rec_inputs():
        import jax
        import jax.numpy as jnp
        _gk = jax.random.key(seed)
        x = -0.0005207 + 1.001 * jax.random.normal(jax.random.fold_in(_gk, 1), (8192, 128), jnp.float32)
        _a = jax.random.bernoulli(jax.random.fold_in(_gk, 2), 0.000244141, (8192, 8192))
        _a = jnp.logical_or(_a, jnp.swapaxes(_a, -1, -2))
        _a = jnp.logical_or(_a, jnp.eye(8192, dtype=bool))
        _af = _a.astype(jnp.float32)
        adj = _af
        return (x, adj)
    x, adj = _rec_inputs()

    def _L0_gnn_setup():
        import jax, jax.numpy as jnp
        import numpy as np
        NEG_INF = -9000000000000000.0
        ALPHA = 0.2
        key = jax.random.key(seed)
        ks = jax.random.split(key, 8)
        N, F = (4096, 128)
        h = jax.random.normal(ks[0], (N, F), dtype=jnp.float32)
        adj = jax.random.randint(ks[1], (N, N), 0, 2).astype(jnp.float32)
        W = jax.random.normal(ks[2], (F, F), dtype=jnp.float32) * 0.05
        a = jax.random.normal(ks[3], (2 * F, 1), dtype=jnp.float32) * 0.05
        w_ih = jax.random.normal(ks[4], (3 * F, F), dtype=jnp.float32) * 0.05
        w_hh = jax.random.normal(ks[5], (3 * F, F), dtype=jnp.float32) * 0.05
        b_ih = jax.random.normal(ks[6], (3 * F,), dtype=jnp.float32) * 0.05
        b_hh = jax.random.normal(ks[7], (3 * F,), dtype=jnp.float32) * 0.05
        return {'h': h, 'adj': adj, 'W': W, 'a': a, 'w_ih': w_ih, 'w_hh': w_hh, 'b_ih': b_ih, 'b_hh': b_hh}
    _L0_gnn_all = _L0_gnn_setup()
    _L0_gnn_in = {k: v for k, v in _L0_gnn_all.items() if k in ('W', 'a', 'w_ih', 'w_hh', 'b_ih', 'b_hh')}
    del _L0_gnn_all

    def _L1_gnn_setup():
        import jax, jax.numpy as jnp
        import numpy as np
        N_NODES = 8192
        D_FEAT = 128
        key = jax.random.key(seed)
        k1, k2, k3 = jax.random.split(key, 3)
        x = jax.random.normal(k1, (N_NODES, D_FEAT), dtype=jnp.float32)
        adj_matrix = jax.random.uniform(k2, (N_NODES, N_NODES), dtype=jnp.float32) / N_NODES
        W = jax.random.normal(k3, (D_FEAT, D_FEAT), dtype=jnp.float32) / np.sqrt(D_FEAT)
        b = jnp.zeros((D_FEAT,), dtype=jnp.float32)
        return {'x': x, 'adj_matrix': adj_matrix, 'W': W, 'b': b}
    _L1_gnn_all = _L1_gnn_setup()
    _L1_gnn_in = {k: v for k, v in _L1_gnn_all.items() if k in ('W', 'b')}
    del _L1_gnn_all
    return {'x': x, 'adj': adj, 'L0_gnn_W': _L0_gnn_in['W'], 'L0_gnn_a': _L0_gnn_in['a'], 'L0_gnn_w_ih': _L0_gnn_in['w_ih'], 'L0_gnn_w_hh': _L0_gnn_in['w_hh'], 'L0_gnn_b_ih': _L0_gnn_in['b_ih'], 'L0_gnn_b_hh': _L0_gnn_in['b_hh'], 'L1_gnn_W': _L1_gnn_in['W'], 'L1_gnn_b': _L1_gnn_in['b']}

def reference(x, adj, L0_gnn_W, L0_gnn_a, L0_gnn_w_ih, L0_gnn_w_hh, L0_gnn_b_ih, L0_gnn_b_hh, L1_gnn_W, L1_gnn_b):
    import jax
    import jax.numpy as jnp

    def _L0_gnn_ref(h, adj, W, a, w_ih, w_hh, b_ih, b_hh):
        import jax, jax.numpy as jnp
        import numpy as np
        NEG_INF = -9000000000000000.0
        ALPHA = 0.2
        F_out = W.shape[1]
        Wh = h @ W
        src = Wh @ a[:F_out]
        dst = Wh @ a[F_out:]
        e = jax.nn.leaky_relu(src + dst.T, ALPHA)
        att = jnp.where(adj > 0, e, NEG_INF)
        att = jax.nn.softmax(att, axis=1)
        h_prime = att @ Wh
        gi = h_prime @ w_ih.T + b_ih
        gh = h @ w_hh.T + b_hh
        i_r, i_z, i_n = jnp.split(gi, 3, axis=1)
        h_r, h_z, h_n = jnp.split(gh, 3, axis=1)
        r = jax.nn.sigmoid(i_r + h_r)
        z = jax.nn.sigmoid(i_z + h_z)
        n = jnp.tanh(i_n + r * h_n)
        return (1.0 - z) * n + z * h

    def _L1_gnn_ref(x, adj_matrix, W, b):
        import jax, jax.numpy as jnp
        import numpy as np
        N_NODES = 8192
        D_FEAT = 128
        h = jnp.einsum('nd,ed->ne', x, W) + b
        return jnp.matmul(adj_matrix, h)
    h = jnp.maximum(_layernorm(x, axis=-1), 0.0)
    x = x + _L0_gnn_ref(h, adj, L0_gnn_W, L0_gnn_a, L0_gnn_w_ih, L0_gnn_w_hh, L0_gnn_b_ih, L0_gnn_b_hh)
    h = jnp.maximum(_layernorm(x, axis=-1), 0.0)
    x = x + _L1_gnn_ref(h, adj, L1_gnn_W, L1_gnn_b)
    return x

_drawn_inputs = setup_inputs


def setup_inputs(seed=0):
    import zlib

    import numpy as np

    out = dict(_drawn_inputs(seed))
    spreads = {'L1_gnn_b': (0.0, 0.1)}
    factors = {'L0_gnn_a': 8.0, 'L0_gnn_b_hh': 4.693}
    for name, (base, spread) in spreads.items():
        noise = np.random.default_rng([zlib.crc32(name.encode()), seed]).standard_normal(out[name].shape)
        drawn = base * np.exp(spread * noise) if base else spread * noise
        out[name] = jnp.asarray(drawn.astype(out[name].dtype))
    for name, factor in factors.items():
        out[name] = (out[name] * factor).astype(out[name].dtype)
    return out
```

```python
from contextlib import ExitStack

import concourse.bass as bass
from concourse import mybir

N = 8192
F = 128
P = 128
NT = N // P
CH = 2048
NC = N // CH
GC = 512
NG = N // GC
CREDIT = 1
SLOPE = 0.2
NEG = 9000000000000000.0
EPS = 1e-5

f32 = mybir.dt.float32
ALU = mybir.AluOpType
ACT = mybir.ActivationFunctionType
AX = mybir.AxisListType


def general_path(nc, x, adj, w, a, w_ih, w_hh, b_ih, b_hh, w1, b1, out):
    x_t = x.rearrange("(t p) f -> t p f", p=P)
    out_t = out.rearrange("(t p) f -> t p f", p=P)
    adj_t = adj.rearrange("(t p) n -> t p n", p=P)

    ctx = ExitStack()
    with ctx:
        def sb(name, shape, dt=f32):
            return ctx.enter_context(nc.sbuf_tensor("g_" + name, shape, dt))

        def ps(name):
            return ctx.enter_context(nc.psum_tensor("g_" + name, [P, 512], f32))

        def sem(name):
            return ctx.enter_context(nc.semaphore("g_" + name))

        H = sb("H", [P, NT, F])
        WH = sb("WH", [P, NT, F + 2])
        DB = sb("DB", [P, N])
        G = sb("G", [P, NT, F])
        A = [sb(f"A{b}", [P, CH]) for b in range(2)]
        T1 = sb("T1", [P, CH])
        Z = sb("Z", [P, N])
        PT = [sb(f"PT{b}", [P, GC]) for b in range(2)]
        ident = sb("ident", [P, P])
        ones = sb("ones", [1, P])
        wext = sb("wext", [P, F + 2])
        wab = sb("wab", [P, P])
        wT = sb("wT", [P, F])
        w1T = sb("w1T", [P, F])
        acol = sb("acol", [P, 2])
        wihT = sb("wihT", [P, 3 * F])
        whhT = sb("whhT", [P, 3 * F])
        raw = Z[:, 0:7 * F].rearrange("p (c f) -> p c f", f=F)
        brow = T1[0:1, 0:7 * F]
        bsum = T1[0:1, 7 * F:9 * F]
        bias = sb("bias", [P, 4 * F])
        b1b = sb("b1b", [P, F])
        epst = sb("epst", [P, 1])
        stat = sb("stat", [P, 6])
        mv = sb("mv", [P, 2])
        std = sb("std", [P, 1])
        rstd = sb("rstd", [P, 1])
        hs = sb("hs", [P, F])
        xt = sb("xt", [P, F])
        hp = sb("hp", [P, F])
        gT = sb("gT", [P, 2 * F])
        gs = sb("gs", [P, 4 * F])
        rz = sb("rz", [P, 2 * F])
        nn = sb("nn", [P, F])
        tmp = sb("tmp", [P, F])
        nmax = sb("nmax", [P, 1])
        rsum = sb("rsum", [P, 1])
        rden = sb("rden", [P, 1])
        ot = sb("ot", [P, F])

        TP = [ps(f"TP{b}") for b in range(2)]
        TG = ps("TG")
        GP = ps("GP")
        OP = ps("OP")

        s_in, s_id, s_tr, s_cp, s_v = (sem(n) for n in ("w_in", "w_id", "w_tr", "w_cp", "w_v"))
        with nc.Block() as block:
            @block.sync
            def _(sp):
                sp.dma_start(H[:, :, :], x.rearrange("(t p) f -> p t f", p=P)).then_inc(s_in, 16)
                sp.dma_start(raw[:, 0, :], w).then_inc(s_in, 16)
                sp.dma_start(raw[:, 1:4, :], w_ih.rearrange("(c p) f -> p c f", p=P)).then_inc(s_in, 16)
                sp.dma_start(raw[:, 4:7, :], w_hh.rearrange("(c p) f -> p c f", p=P)).then_inc(s_in, 16)
                sp.dma_start(w1T[:, :], w1).then_inc(s_in, 16)
                for c in range(2):
                    sp.dma_start(acol[:, c:c + 1], a[c * F:(c + 1) * F, :]).then_inc(s_in, 16)
                sp.dma_start(brow[0:1, 0:3 * F], b_ih.rearrange("(o n) -> o n", o=1)).then_inc(s_in, 16)
                sp.dma_start(brow[0:1, 3 * F:6 * F], b_hh.rearrange("(o n) -> o n", o=1)).then_inc(s_in, 16)
                sp.dma_start(brow[0:1, 6 * F:7 * F], b1.rearrange("(o n) -> o n", o=1)).then_inc(s_in, 16)

            @block.gpsimd
            def _(pool):
                nc.gpsimd.memset(ident[:, :], 0.0).then_inc(s_id, 1)
                nc.gpsimd.memset(ones[:, :], 1.0).then_inc(s_id, 1)
                nc.gpsimd.memset(epst[:, :], EPS).then_inc(s_id, 1)
                pool.wait_ge(s_id, 3)
                nc.gpsimd.affine_select(out=ident[:, :], in_=ident[:, :], compare_op=ALU.not_equal, fill=1.0,
                                        base=0, pattern=[[-1, P]], channel_multiplier=1).then_inc(s_id, 1)

            @block.tensor
            def _(pe):
                pe.wait_ge(s_in, 160)
                pe.wait_ge(s_id, 4)
                for k in range(8):
                    src = raw[:, k, :] if k < 7 else w1T[:, :]
                    bank = (TP[0], TP[1])[k // 4]
                    ins = nc.tensor.transpose(bank[:, (k % 4) * F:(k % 4 + 1) * F], src, ident[:, :])
                ins.then_inc(s_tr, 1)
                pe.wait_ge(s_cp, 4)
                nc.tensor.matmul(TG[:, 0:2], wT[:, :], acol[:, :], start=True, stop=True).then_inc(s_tr, 1)
                pe.wait_ge(s_v, 1)
                nc.tensor.matmul(GP[:, 0:2 * F], ones[:, :], bsum[0:1, :], start=True, stop=True)
                nc.tensor.matmul(GP[:, 2 * F:3 * F], ones[:, :], brow[0:1, 2 * F:3 * F], start=True, stop=True)
                nc.tensor.matmul(GP[:, 3 * F:4 * F], ones[:, :], brow[0:1, 5 * F:6 * F], start=True, stop=True)
                nc.tensor.matmul(OP[:, 0:F], ones[:, :], brow[0:1, 6 * F:7 * F], start=True,
                                 stop=True).then_inc(s_tr, 1)

            @block.vector
            def _(dve):
                dve.wait_ge(s_in, 160)
                nc.vector.tensor_tensor(bsum[0:1, :], brow[0:1, 0:2 * F], brow[0:1, 3 * F:5 * F], ALU.add).then_inc(s_v, 1)
                dve.wait_ge(s_tr, 1)
                nc.vector.tensor_copy(wT[:, :], TP[0][:, 0:F]).then_inc(s_cp, 1)
                nc.vector.tensor_copy(wihT[:, :], TP[0][:, F:4 * F]).then_inc(s_cp, 1)
                nc.vector.tensor_copy(whhT[:, :], TP[1][:, 0:3 * F]).then_inc(s_cp, 1)
                nc.vector.tensor_copy(w1T[:, :], TP[1][:, 3 * F:4 * F]).then_inc(s_cp, 1)
                nc.vector.tensor_copy(wext[:, 0:F], raw[:, 0, :]).then_inc(s_v, 1)
                dve.wait_ge(s_tr, 2)
                nc.vector.tensor_copy(wext[:, F:F + 2], TG[:, 0:2]).then_inc(s_v, 1)
                nc.vector.tensor_copy(wab[:, :], TG[:, 1:2].to_broadcast([P, P])).then_inc(s_v, 1)
                dve.wait_ge(s_tr, 3)
                nc.vector.tensor_copy(bias[:, :], GP[:, :]).then_inc(s_v, 1)
                nc.vector.tensor_copy(b1b[:, :], OP[:, 0:F]).then_inc(s_v, 1)

        n_dve, n_std, n_hs, n_tr, n_hT, n_mm, n_wh = (
            sem(n) for n in ("n_dve", "n_std", "n_hs", "n_tr", "n_hT", "n_mm", "n_wh"))
        with nc.Block() as block:
            @block.vector
            def _(dve):
                dve.sem_inc(n_wh, CREDIT)
                with dve.Fori(0, NT) as t:
                    nc.vector.bn_stats(stat[:, :], H[:, t, :]).then_inc(n_dve, 1)
                    dve.drain()
                    nc.vector.bn_aggr(mv[:, :], stat[:, :]).then_inc(n_dve, 1)
                    dve.wait_ge(n_std, t + 1)
                    nc.vector.reciprocal(rstd[:, :], std[:, :]).then_inc(n_dve, 1)
                    dve.wait_ge(n_dve, t * 4 + 3)
                    dve.wait_ge(n_tr, CREDIT + t)
                    nc.vector.tensor_scalar(hs[:, :], H[:, t, :], mv[:, 0:1], rstd[:, :], ALU.subtract,
                                            ALU.mult).then_inc(n_dve, 1)
                    dve.wait_ge(n_dve, t * 4 + 4)
                    nc.vector.tensor_scalar(hs[:, :], hs[:, :], 0.0, None, ALU.max).then_inc(n_hs, 1)
                    dve.wait_ge(n_hs, t + 1)
                    nc.vector.tensor_scalar(H[:, t, :], hs[:, :], 1.0, None, ALU.mult)
                    dve.wait_ge(n_mm, CREDIT + t + 1)
                    nc.vector.tensor_scalar(WH[:, t, :], GP[:, 0:F + 2], 1.0, None, ALU.mult)
                    nc.vector.tensor_copy(DB[:, bass.ts(t, P)], GP[:, 2 * F:3 * F]).then_inc(n_wh, 1)

            @block.scalar
            def _(act):
                act.sem_inc(n_hT, CREDIT)
                with act.Fori(0, NT) as t:
                    act.wait_ge(n_dve, t * 4 + 2)
                    nc.scalar.activation(std[:, :], mv[:, 1:2], ACT.Sqrt, bias=epst[:, :]).then_inc(n_std, 1)
                    act.wait_ge(n_tr, CREDIT + t + 1)
                    act.wait_ge(n_mm, CREDIT + t)
                    nc.scalar.activation(gT[:, 0:F], TG[:, 0:F], ACT.Copy).then_inc(n_hT, 1)

            @block.tensor
            def _(pe):
                pe.sem_inc(n_tr, CREDIT)
                pe.sem_inc(n_mm, CREDIT)
                with pe.Fori(0, NT) as t:
                    pe.wait_ge(n_hs, t + 1)
                    pe.wait_ge(n_hT, CREDIT + t)
                    nc.tensor.transpose(TG[:, 0:F], hs[:, :], ident[:, :]).then_inc(n_tr, 1)
                    pe.wait_ge(n_hT, CREDIT + t + 1)
                    pe.wait_ge(n_wh, CREDIT + t)
                    nc.tensor.matmul(GP[:, 0:F + 2], gT[:, 0:F], wext[:, :], start=True, stop=True)
                    nc.tensor.matmul(GP[:, 2 * F:3 * F], wab[:, :], gT[:, 0:F], start=True,
                                     stop=True).then_inc(n_mm, 1)

        a_in = [sem(f"a_in{b}") for b in range(2)]
        a_z = [sem(f"a_z{b}") for b in range(2)]
        a_x, a_t1, a_e, a_m, a_max, a_p = (sem(n) for n in ("a_x", "a_t1", "a_e", "a_m", "a_max", "a_p"))
        a_tr = [sem(f"a_tr{b}") for b in range(2)]
        a_pt = [sem(f"a_pt{b}") for b in range(2)]
        a_mm = [sem(f"a_mm{b}") for b in range(2)]
        a_step, a_act, a_pe = sem("a_step"), sem("a_act"), sem("a_pe")
        KV, KA, KP = 15, 5, 4
        with nc.Block() as block:
            @block.sync
            def _(sp):
                with sp.Fori(0, NT) as t:
                    for c in range(NC):
                        b = c % 2
                        sp.wait_ge(a_z[b], CREDIT + t * (NC // 2) + c // 2)
                        sp.dma_start(A[b][:, :], adj_t[t, :, c * CH:(c + 1) * CH]).then_inc(a_in[b], 16)
                    sp.wait_ge(a_step, CREDIT + t * KV)
                    sp.dma_start(xt[:, :], x_t[t, :, :]).then_inc(a_x, 16)

            @block.scalar
            def _(act):
                act.sem_inc(a_pt[0], CREDIT)
                act.sem_inc(a_pt[1], CREDIT)
                with act.Fori(0, NT) as t:
                    act.wait_ge(a_max, t + 1)
                    nc.scalar.activation(Z[:, :], Z[:, :], ACT.Exp, bias=nmax[:, :],
                                         accum_out=rsum[:, :]).then_inc(a_p, 1)
                    for c in range(NG):
                        b = c % 2
                        act.wait_ge(a_tr[b], CREDIT + t * (NG // 2) + c // 2 + 1)
                        act.wait_ge(a_mm[b], CREDIT + t * (NG // 2) + c // 2)
                        nc.scalar.activation(PT[b][:, :], TP[b][:, :], ACT.Copy).then_inc(a_pt[b], 1)
                    act.wait_ge(a_pe, t * KP + 1)
                    nc.scalar.activation(gT[:, :], TG[:, 0:2 * F], ACT.Copy).then_inc(a_act, 1)
                    act.wait_ge(a_step, CREDIT + t * KV + 4)
                    nc.scalar.activation(rz[:, :], gs[:, 0:2 * F], ACT.Sigmoid).then_inc(a_act, 1)
                    act.wait_ge(a_step, CREDIT + t * KV + 6)
                    nc.scalar.activation(nn[:, :], tmp[:, :], ACT.Tanh).then_inc(a_act, 1)
                    act.wait_ge(a_step, CREDIT + t * KV + 12)
                    nc.scalar.activation(std[:, :], mv[:, 1:2], ACT.Sqrt, bias=epst[:, :]).then_inc(a_act, 1)
                    act.wait_ge(a_pe, t * KP + 3)
                    nc.scalar.activation(gT[:, 0:F], TG[:, 0:F], ACT.Copy).then_inc(a_act, 1)

            @block.vector
            def _(dve):
                dve.sem_inc(a_z[0], CREDIT)
                dve.sem_inc(a_z[1], CREDIT)
                dve.sem_inc(a_e, CREDIT)
                dve.sem_inc(a_step, CREDIT)
                with dve.Fori(0, NT) as t:
                    for c in range(NC):
                        b = c % 2
                        dve.wait_ge(a_in[b], (t * (NC // 2) + c // 2 + 1) * 16)
                        nc.vector.tensor_scalar(A[b][:, :], A[b][:, :], 0.0, 1.0, ALU.is_gt,
                                                ALU.subtract).then_inc(a_m, 1)
                        dve.wait_ge(a_e, CREDIT + t * NC + c)
                        nc.vector.tensor_scalar(T1[:, :], DB[:, c * CH:(c + 1) * CH], WH[:, t, F:F + 1], None,
                                                ALU.add).then_inc(a_t1, 1)
                        dve.wait_ge(a_t1, t * NC + c + 1)
                        if c == 0:
                            dve.wait_ge(a_tr[0], CREDIT + t * (NG // 2))
                            dve.wait_ge(a_tr[1], CREDIT + t * (NG // 2))
                        z = Z[:, c * CH:(c + 1) * CH]
                        nc.vector.scalar_tensor_tensor(z, T1[:, :], SLOPE, T1[:, :], ALU.mult,
                                                       ALU.max).then_inc(a_e, 1)
                        dve.wait_ge(a_m, t * NC + c + 1)
                        dve.wait_ge(a_e, CREDIT + t * NC + c + 1)
                        nc.vector.scalar_tensor_tensor(z, A[b][:, :], NEG, z, ALU.mult,
                                                       ALU.add).then_inc(a_z[b], 1)
                    for b in range(2):
                        dve.wait_ge(a_z[b], CREDIT + (t + 1) * (NC // 2))
                    nc.vector.tensor_reduce(nmax[:, :], Z[:, :], AX.X, ALU.max).then_inc(a_step, 1)
                    dve.wait_ge(a_step, CREDIT + t * KV + 1)
                    nc.vector.tensor_scalar(nmax[:, :], nmax[:, :], -1.0, None, ALU.mult).then_inc(a_max, 1)
                    dve.wait_ge(a_p, t + 1)
                    nc.vector.reciprocal(rden[:, :], rsum[:, :]).then_inc(a_step, 1)
                    dve.wait_ge(a_step, CREDIT + t * KV + 2)
                    nc.vector.tensor_scalar(hs[:, :], H[:, t, :], 1.0, None, ALU.mult)
                    dve.wait_ge(a_mm[1], CREDIT + (t + 1) * (NG // 2))
                    nc.vector.tensor_scalar(hp[:, :], OP[:, 0:F], rden[:, :], None, ALU.mult).then_inc(a_step, 1)
                    dve.wait_ge(a_pe, t * KP + 2)
                    nc.vector.tensor_tensor(gs[:, :], GP[:, :], bias[:, :], ALU.add).then_inc(a_step, 1)
                    dve.wait_ge(a_step, CREDIT + t * KV + 4)
                    dve.wait_ge(a_act, t * KA + 2)
                    nc.vector.tensor_tensor(tmp[:, :], rz[:, 0:F], gs[:, 3 * F:4 * F], ALU.mult).then_inc(a_step, 1)
                    dve.wait_ge(a_step, CREDIT + t * KV + 5)
                    nc.vector.tensor_tensor(tmp[:, :], tmp[:, :], gs[:, 2 * F:3 * F], ALU.add).then_inc(a_step, 1)
                    dve.wait_ge(a_act, t * KA + 3)
                    nc.vector.tensor_tensor(tmp[:, :], hs[:, :], nn[:, :], ALU.subtract).then_inc(a_step, 1)
                    dve.wait_ge(a_step, CREDIT + t * KV + 7)
                    nc.vector.tensor_tensor(tmp[:, :], tmp[:, :], rz[:, F:2 * F], ALU.mult).then_inc(a_step, 1)
                    dve.wait_ge(a_step, CREDIT + t * KV + 8)
                    nc.vector.tensor_tensor(tmp[:, :], tmp[:, :], nn[:, :], ALU.add).then_inc(a_step, 1)
                    dve.wait_ge(a_step, CREDIT + t * KV + 9)
                    dve.wait_ge(a_x, (t + 1) * 16)
                    nc.vector.tensor_tensor(tmp[:, :], tmp[:, :], xt[:, :], ALU.add).then_inc(a_step, 1)
                    dve.wait_ge(a_step, CREDIT + t * KV + 10)
                    nc.vector.tensor_scalar(H[:, t, :], tmp[:, :], 1.0, None, ALU.mult)
                    nc.vector.bn_stats(stat[:, :], tmp[:, :]).then_inc(a_step, 1)
                    dve.drain()
                    nc.vector.bn_aggr(mv[:, :], stat[:, :]).then_inc(a_step, 1)
                    dve.wait_ge(a_act, t * KA + 4)
                    nc.vector.reciprocal(rstd[:, :], std[:, :]).then_inc(a_step, 1)
                    dve.wait_ge(a_step, CREDIT + t * KV + 13)
                    nc.vector.tensor_scalar(hp[:, :], tmp[:, :], mv[:, 0:1], rstd[:, :], ALU.subtract,
                                            ALU.mult).then_inc(a_step, 1)
                    dve.wait_ge(a_step, CREDIT + t * KV + 14)
                    nc.vector.tensor_scalar(hp[:, :], hp[:, :], 0.0, None, ALU.max).then_inc(a_step, 1)
                    dve.wait_ge(a_pe, t * KP + 4)
                    nc.vector.tensor_tensor(G[:, t, :], GP[:, 0:F], b1b[:, :], ALU.add)

            @block.tensor
            def _(pe):
                pe.sem_inc(a_tr[0], CREDIT)
                pe.sem_inc(a_tr[1], CREDIT)
                pe.sem_inc(a_mm[0], CREDIT)
                pe.sem_inc(a_mm[1], CREDIT)
                with pe.Fori(0, NT) as t:
                    def product(c):
                        b = c % 2
                        pe.wait_ge(a_pt[b], CREDIT + t * (NG // 2) + c // 2 + 1)
                        for k in range(4):
                            j = 4 * c + k
                            ins = nc.tensor.matmul(OP[:, 0:F], PT[b][:, k * P:(k + 1) * P], WH[:, j, 0:F],
                                                   start=(j == 0), stop=(j == NT - 1))
                        ins.then_inc(a_mm[b], 1)

                    pe.wait_ge(a_p, t + 1)
                    for c in range(NG):
                        b = c % 2
                        if c < 2:
                            pe.wait_ge(a_pt[b], CREDIT + t * (NG // 2))
                        for k in range(4):
                            j = 4 * c + k
                            ins = nc.tensor.transpose(TP[b][:, k * P:(k + 1) * P], Z[:, j * P:(j + 1) * P],
                                                      ident[:, :])
                        ins.then_inc(a_tr[b], 1)
                        if c >= 1:
                            product(c - 1)
                    product(NG - 1)
                    pe.wait_ge(a_step, CREDIT + t * KV + 3)
                    nc.tensor.transpose(TG[:, 0:F], hp[:, :], ident[:, :])
                    nc.tensor.transpose(TG[:, F:2 * F], hs[:, :], ident[:, :]).then_inc(a_pe, 1)
                    pe.wait_ge(a_act, t * KA + 1)
                    nc.tensor.matmul(GP[:, 0:3 * F], gT[:, 0:F], wihT[:, :], start=True, stop=False)
                    nc.tensor.matmul(GP[:, 0:2 * F], gT[:, F:2 * F], whhT[:, 0:2 * F], start=False, stop=False)
                    nc.tensor.matmul(GP[:, 3 * F:4 * F], gT[:, F:2 * F], whhT[:, 2 * F:3 * F], start=False,
                                     stop=True).then_inc(a_pe, 1)
                    pe.wait_ge(a_step, CREDIT + t * KV + 15)
                    nc.tensor.transpose(TG[:, 0:F], hp[:, :], ident[:, :]).then_inc(a_pe, 1)
                    pe.wait_ge(a_act, t * KA + 5)
                    nc.tensor.matmul(GP[:, 0:F], gT[:, 0:F], w1T[:, :], start=True, stop=True).then_inc(a_pe, 1)

        l_in = [sem(f"l_in{b}") for b in range(2)]
        l_tr = [sem(f"l_tr{b}") for b in range(2)]
        l_pt = [sem(f"l_pt{b}") for b in range(2)]
        l_mm = [sem(f"l_mm{b}") for b in range(2)]
        l_o, l_out = sem("l_o"), sem("l_out")
        GPC = CH // GC
        with nc.Block() as block:
            @block.sync
            def _(sp):
                with sp.Fori(0, NT) as t:
                    for c in range(NC):
                        b = c % 2
                        done = t * (NG // 2) if c < 2 else t * (NG // 2) + (c - 1) * (GPC // 2)
                        sp.wait_ge(l_tr[1], CREDIT + done)
                        sp.dma_start(A[b][:, :], adj_t[t, :, c * CH:(c + 1) * CH]).then_inc(l_in[b], 16)
                    sp.wait_ge(l_o, CREDIT + t + 1)
                    sp.dma_start(out_t[t, :, :], ot[:, :]).then_inc(l_out, 16)
                sp.wait_ge(l_out, NT * 16)

            @block.tensor
            def _(pe):
                pe.sem_inc(l_tr[0], CREDIT)
                pe.sem_inc(l_tr[1], CREDIT)
                pe.sem_inc(l_mm[0], CREDIT)
                pe.sem_inc(l_mm[1], CREDIT)
                with pe.Fori(0, NT) as t:
                    def product(c):
                        b = c % 2
                        pe.wait_ge(l_pt[b], CREDIT + t * (NG // 2) + c // 2 + 1)
                        if c == 0:
                            pe.wait_ge(l_o, CREDIT + t)
                        for k in range(4):
                            j = 4 * c + k
                            ins = nc.tensor.matmul(OP[:, 0:F], PT[b][:, k * P:(k + 1) * P], G[:, j, :],
                                                   start=(j == 0), stop=(j == NT - 1))
                        ins.then_inc(l_mm[b], 1)

                    for c in range(NG):
                        b = c % 2
                        if c % GPC == 0:
                            q = c // GPC
                            pe.wait_ge(l_in[q % 2], (t * (NC // 2) + q // 2 + 1) * 16)
                        pe.wait_ge(l_pt[b], CREDIT + t * (NG // 2) + c // 2)
                        for k in range(4):
                            j = (c % GPC) * 4 + k
                            ins = nc.tensor.transpose(TP[b][:, k * P:(k + 1) * P],
                                                      A[(c // GPC) % 2][:, j * P:(j + 1) * P], ident[:, :])
                        ins.then_inc(l_tr[b], 1)
                        if c >= 1:
                            product(c - 1)
                    product(NG - 1)

            @block.scalar
            def _(act):
                act.sem_inc(l_pt[0], CREDIT)
                act.sem_inc(l_pt[1], CREDIT)
                with act.Fori(0, NT) as t:
                    for c in range(NG):
                        b = c % 2
                        act.wait_ge(l_tr[b], CREDIT + t * (NG // 2) + c // 2 + 1)
                        act.wait_ge(l_mm[b], CREDIT + t * (NG // 2) + c // 2)
                        nc.scalar.activation(PT[b][:, :], TP[b][:, :], ACT.Copy).then_inc(l_pt[b], 1)

            @block.vector
            def _(dve):
                dve.sem_inc(l_o, CREDIT)
                with dve.Fori(0, NT) as t:
                    dve.wait_ge(l_mm[1], CREDIT + (t + 1) * (NG // 2))
                    nc.vector.tensor_tensor(ot[:, :], OP[:, 0:F], H[:, t, :], ALU.add).then_inc(l_o, 1)
                    dve.wait_ge(l_out, (t + 1) * 16)


_INS = ['x', 'adj', 'L0_gnn_W', 'L0_gnn_a', 'L0_gnn_w_ih', 'L0_gnn_w_hh', 'L0_gnn_b_ih', 'L0_gnn_b_hh',
        'L1_gnn_W', 'L1_gnn_b']
_OUTS = [((8192, 128), 'float32')]


def kernel(**inputs):
    import numpy as _np
    import concourse.bacc as _bacc
    from concourse import mybir as _mybir
    from concourse.bass_utils import run_bass_kernel_spmd as _run

    nc = _bacc.Bacc("TRN2", target_bir_lowering=False, num_devices=1)
    arrays, args = {}, []
    for name in _INS:
        arr = _np.ascontiguousarray(inputs[name])
        arrays[f"in_{name}_dram"] = arr
        args.append(nc.dram_tensor(f"in_{name}_dram", arr.shape, _mybir.dt.from_np(arr.dtype),
                                   kind="ExternalInput").ap())
    for i, (shape, dtype) in enumerate(_OUTS):
        dt = _mybir.dt.from_np(_np.dtype(dtype))
        args.append(nc.dram_tensor(f"out_{i}_dram", shape, dt, kind="ExternalOutput").ap())
    general_path(nc, *args)
    r = _run(nc, [arrays], core_ids=[0])
    return r.results[0]["out_0_dram"]
```

```python
from contextlib import ExitStack

import concourse.bass as bass
from concourse import mybir

N = 8192
F = 128
P = 128
NT = N // P
CH = 2048
NC = N // CH
GC = 512
NG = N // GC
GPC = CH // GC
NB = 4
LAG = 2
CREDIT = 1
SLOPE = 0.2
NEG = 9000000000000000.0
LEAST = -3.0e38
EPS = 1e-5

f32 = mybir.dt.float32
ALU = mybir.AluOpType
ACT = mybir.ActivationFunctionType
AX = mybir.AxisListType


def graph_layers(nc, x, adj, w, a, w_ih, w_hh, b_ih, b_hh, w1, b1, out):
    x_t = x.rearrange("(t p) f -> t p f", p=P)
    out_t = out.rearrange("(t p) f -> t p f", p=P)
    adj_t = adj.rearrange("(t p) n -> t p n", p=P)

    ctx = ExitStack()
    with ctx:
        def sb(name, shape, dt=f32):
            return ctx.enter_context(nc.sbuf_tensor(name, shape, dt))

        def ps(name):
            return ctx.enter_context(nc.psum_tensor(name, [P, 512], f32))

        def sem(name):
            return ctx.enter_context(nc.semaphore(name))

        H = sb("H", [P, NT, F])
        WH = sb("WH", [P, NT, F + 2])
        DB = sb("DB", [P, N])
        A = [sb(f"A{b}", [P, CH]) for b in range(2)]
        Z = [sb(f"Z{b}", [P, N]) for b in range(2)]
        PT = [sb(f"PT{b}", [P, GC]) for b in range(NB)]
        ident = sb("ident", [P, P])
        ones = sb("ones", [1, P])
        wext = sb("wext", [P, F + 2])
        wab = sb("wab", [P, P])
        wT = sb("wT", [P, F])
        w1T = sb("w1T", [P, F])
        acol = sb("acol", [P, 2])
        wihT = sb("wihT", [P, 3 * F])
        whhT = sb("whhT", [P, 3 * F])
        raw = Z[0][:, 0:7 * F].rearrange("p (c f) -> p c f", f=F)
        brow = Z[1][0:1, 0:7 * F]
        bsum = Z[1][0:1, 7 * F:9 * F]
        bias = sb("bias", [P, 4 * F])
        b1b = sb("b1b", [P, F])
        epst = sb("epst", [P, 1])
        stat = sb("stat", [P, 6])
        mv = sb("mv", [P, 2])
        rstd = sb("rstd", [P, 1])
        hs = sb("hs", [P, F])
        xt = sb("xt", [P, F])
        hp = sb("hp", [P, F])
        gT = sb("gT", [P, 2 * F])
        gs = sb("gs", [P, 4 * F])
        rz = sb("rz", [P, 2 * F])
        nn = sb("nn", [P, F])
        tmp = sb("tmp", [P, F])
        x1s = sb("x1s", [P, F])
        xp = sb("xp", [P, F])
        ve = sb("ve", [P, 1])
        half = sb("half", [P, 1])
        scol = sb("scol", [P, 1])
        mx4 = sb("mx4", [P, NC])
        mx = sb("mx", [P, 1])
        mxs = sb("mxs", [P, 1])
        nm = sb("nm", [P, 1])
        rs = [sb(f"rs{b}", [P, NC]) for b in range(2)]
        rsum = sb("rsum", [P, 1])
        rden = sb("rden", [P, 1])
        x1_dram = nc.dram_tensor("x_after_layer_0", [N, F], f32)
        x1_t = x1_dram.ap().rearrange("(t p) f -> t p f", p=P)

        TP = [ps(f"TP{b}") for b in range(NB)]
        TG = ps("TG")
        GP = ps("GP")
        OP = ps("OP")
        OQ = ps("OQ")
        ACC = [OP, OQ]

        s_in, s_id, s_tr, s_cp, s_v = (sem(n) for n in ("w_in", "w_id", "w_tr", "w_cp", "w_v"))
        with nc.Block() as block:
            @block.sync
            def _(sp):
                sp.dma_start(H[:, :, :], x.rearrange("(t p) f -> p t f", p=P)).then_inc(s_in, 16)
                sp.dma_start(raw[:, 0, :], w).then_inc(s_in, 16)
                sp.dma_start(raw[:, 1:4, :], w_ih.rearrange("(c p) f -> p c f", p=P)).then_inc(s_in, 16)
                sp.dma_start(raw[:, 4:7, :], w_hh.rearrange("(c p) f -> p c f", p=P)).then_inc(s_in, 16)
                sp.dma_start(w1T[:, :], w1).then_inc(s_in, 16)
                for c in range(2):
                    sp.dma_start(acol[:, c:c + 1], a[c * F:(c + 1) * F, :]).then_inc(s_in, 16)
                sp.dma_start(brow[0:1, 0:3 * F], b_ih.rearrange("(o n) -> o n", o=1)).then_inc(s_in, 16)
                sp.dma_start(brow[0:1, 3 * F:6 * F], b_hh.rearrange("(o n) -> o n", o=1)).then_inc(s_in, 16)
                sp.dma_start(brow[0:1, 6 * F:7 * F], b1.rearrange("(o n) -> o n", o=1)).then_inc(s_in, 16)

            @block.gpsimd
            def _(pool):
                nc.gpsimd.memset(ident[:, :], 0.0).then_inc(s_id, 1)
                nc.gpsimd.memset(ones[:, :], 1.0).then_inc(s_id, 1)
                nc.gpsimd.memset(epst[:, :], EPS).then_inc(s_id, 1)
                nc.gpsimd.memset(half[:, :], -0.5).then_inc(s_id, 1)
                pool.wait_ge(s_id, 4)
                nc.gpsimd.affine_select(out=ident[:, :], in_=ident[:, :], compare_op=ALU.not_equal, fill=1.0,
                                        base=0, pattern=[[-1, P]], channel_multiplier=1).then_inc(s_id, 1)

            @block.tensor
            def _(pe):
                pe.wait_ge(s_in, 160)
                pe.wait_ge(s_id, 5)
                for k in range(8):
                    src = raw[:, k, :] if k < 7 else w1T[:, :]
                    bank = (TP[0], TP[1])[k // 4]
                    ins = nc.tensor.transpose(bank[:, (k % 4) * F:(k % 4 + 1) * F], src, ident[:, :])
                ins.then_inc(s_tr, 1)
                pe.wait_ge(s_cp, 4)
                nc.tensor.matmul(TG[:, 0:2], wT[:, :], acol[:, :], start=True, stop=True).then_inc(s_tr, 1)
                pe.wait_ge(s_v, 1)
                nc.tensor.matmul(GP[:, 0:2 * F], ones[:, :], bsum[0:1, :], start=True, stop=True)
                nc.tensor.matmul(GP[:, 2 * F:3 * F], ones[:, :], brow[0:1, 2 * F:3 * F], start=True, stop=True)
                nc.tensor.matmul(GP[:, 3 * F:4 * F], ones[:, :], brow[0:1, 5 * F:6 * F], start=True, stop=True)
                nc.tensor.matmul(OP[:, 0:F], ones[:, :], brow[0:1, 6 * F:7 * F], start=True,
                                 stop=True).then_inc(s_tr, 1)

            @block.vector
            def _(dve):
                dve.wait_ge(s_in, 160)
                nc.vector.tensor_tensor(bsum[0:1, :], brow[0:1, 0:2 * F], brow[0:1, 3 * F:5 * F], ALU.add).then_inc(s_v, 1)
                dve.wait_ge(s_tr, 1)
                nc.vector.tensor_copy(wT[:, :], TP[0][:, 0:F]).then_inc(s_cp, 1)
                nc.vector.tensor_copy(wihT[:, :], TP[0][:, F:4 * F]).then_inc(s_cp, 1)
                nc.vector.tensor_copy(whhT[:, :], TP[1][:, 0:3 * F]).then_inc(s_cp, 1)
                nc.vector.tensor_copy(w1T[:, :], TP[1][:, 3 * F:4 * F]).then_inc(s_cp, 1)
                nc.vector.tensor_copy(wext[:, 0:F], raw[:, 0, :]).then_inc(s_v, 1)
                dve.wait_ge(s_tr, 2)
                nc.vector.tensor_copy(wext[:, F:F + 2], TG[:, 0:2]).then_inc(s_v, 1)
                nc.vector.tensor_copy(wab[:, :], TG[:, 1:2].to_broadcast([P, P])).then_inc(s_v, 1)
                dve.wait_ge(s_tr, 3)
                nc.vector.tensor_copy(bias[:, :], GP[:, :]).then_inc(s_v, 1)
                nc.vector.tensor_copy(b1b[:, :], OP[:, 0:F]).then_inc(s_v, 1)

        n_dve, n_std, n_hs, n_tr, n_hT, n_mm, n_wh, n_db = (
            sem(n) for n in ("n_dve", "n_std", "n_hs", "n_tr", "n_hT", "n_mm", "n_wh", "n_db"))
        B = 4
        hb = Z[0][:, 0:B * F]
        hbT = Z[1][:, 0:B * F]
        stb = Z[0][:, 1024:1024 + B * 6].rearrange("p (b k) -> p b k", k=6)
        mvb = Z[0][:, 1088:1088 + B * 2].rearrange("p (b k) -> p b k", k=2)
        sdb = Z[0][:, 1120:1120 + B]
        rsb = Z[0][:, 1152:1152 + B]
        with nc.Block() as block:
            @block.vector
            def _(dve):
                dve.sem_inc(n_dve, CREDIT)
                with dve.Fori(0, NT // B) as k:
                    for b in range(B):
                        nc.vector.bn_stats(stb[:, b, :], H[:, k * B + b, :])
                    dve.drain()
                    for b in range(B):
                        nc.vector.bn_aggr(mvb[:, b, :], stb[:, b, :]).then_inc(n_dve, 1)
                    dve.wait_ge(n_std, k + 1)
                    nc.vector.reciprocal(rsb, sdb).then_inc(n_dve, 1)
                    dve.wait_ge(n_dve, CREDIT + k * 6 + 5)
                    dve.wait_ge(n_tr, CREDIT + k)
                    for b in range(B):
                        ins = nc.vector.tensor_scalar(hb[:, b * F:(b + 1) * F], H[:, k * B + b, :], mvb[:, b, 0:1],
                                                      rsb[:, b:b + 1], ALU.subtract, ALU.mult)
                    ins.then_inc(n_dve, 1)
                    dve.wait_ge(n_dve, CREDIT + k * 6 + 6)
                    nc.vector.tensor_scalar(hb, hb, 0.0, None, ALU.max).then_inc(n_hs, 1)
                    dve.wait_ge(n_hs, k + 1)
                    nc.vector.tensor_scalar(H[:, bass.ts(k, B), :].rearrange("p b f -> p (b f)"), hb, 1.0, None,
                                            ALU.mult)
                    dve.wait_ge(n_mm, CREDIT + k + 1)
                    for half_ in range(2):
                        ins = nc.vector.tensor_scalar(
                            WH[:, bass.ds(k * B + half_ * 2, 2), :].rearrange("p b f -> p (b f)"),
                            (GP, OP)[half_][:, 0:2 * (F + 2)], 1.0, None, ALU.mult)
                    ins.then_inc(n_wh, 1)

            @block.scalar
            def _(act):
                act.sem_inc(n_hT, CREDIT)
                with act.Fori(0, NT // B) as k:
                    act.wait_ge(n_dve, CREDIT + k * 6 + 4)
                    nc.scalar.activation(sdb, mvb[:, :, 1:2].rearrange("p b k -> p (b k)"), ACT.Sqrt,
                                         bias=epst[:, :]).then_inc(n_std, 1)
                    act.wait_ge(n_tr, CREDIT + k + 1)
                    act.wait_ge(n_mm, CREDIT + k)
                    nc.scalar.activation(hbT, TG[:, :], ACT.Copy).then_inc(n_hT, 1)
                    act.wait_ge(n_mm, CREDIT + k + 1)
                    nc.scalar.activation(DB[:, bass.ts(k, B * P)], OQ[:, :], ACT.Copy).then_inc(n_db, 1)

            @block.tensor
            def _(pe):
                pe.sem_inc(n_tr, CREDIT)
                pe.sem_inc(n_mm, CREDIT)
                pe.sem_inc(n_wh, CREDIT)
                pe.sem_inc(n_db, CREDIT)
                with pe.Fori(0, NT // B) as k:
                    pe.wait_ge(n_hs, k + 1)
                    pe.wait_ge(n_hT, CREDIT + k)
                    for b in range(B):
                        ins = nc.tensor.transpose(TG[:, b * F:(b + 1) * F], hb[:, b * F:(b + 1) * F], ident[:, :])
                    ins.then_inc(n_tr, 1)
                    pe.wait_ge(n_hT, CREDIT + k + 1)
                    pe.wait_ge(n_wh, CREDIT + k)
                    pe.wait_ge(n_db, CREDIT + k)
                    for b in range(B):
                        at = (b % 2) * (F + 2)
                        nc.tensor.matmul((GP, OP)[b // 2][:, at:at + F + 2], hbT[:, b * F:(b + 1) * F], wext[:, :],
                                         start=True, stop=True)
                    nc.tensor.matmul(OQ[:, :], wab[:, :], hbT, start=True, stop=True).then_inc(n_mm, 1)

        a_in = [sem(f"a_in{b}") for b in range(2)]
        a_v = [sem(f"a_v{b}") for b in range(2)]
        a_max = sem("a_max")
        a_ms = sem("a_ms")
        a_x = sem("a_x")
        a_l = sem("a_l")
        a_p = sem("a_p")
        a_tr = sem("a_tr")
        a_pt = sem("a_pt")
        a_mm = sem("a_mm")
        g_v, g_a, g_p, g_r = sem("g_v"), sem("g_a"), sem("g_p"), sem("g_r")
        g_q = sem("g_q")
        x_in, x_out = sem("x_in"), sem("x_out")
        KM, KV, KA, KP, KQ = 3, 13, 4, 4, 4

        def wait(eng, s, value):
            if not isinstance(value, int) or value > 0:
                eng.wait_ge(s, value)

        def slots(eng, slot, first, last):
            for T in range(first, 3):
                slot(T, T % 2)
            with eng.Fori(0, (NT - 4) // 2) as k:
                for d in range(3, 5):
                    slot(k * 2 + d, d % 2)
            for T in range(NT - 1, last + 1):
                slot(T, T % 2)

        with nc.Block() as block:
            @block.sync
            def _(sp):
                def slot(T, u):
                    if not (isinstance(T, int) and T >= NT):
                        for c in range(NC):
                            wait(sp, a_v[c % 2], T * 2 + c // 2)
                            sp.dma_start(A[c % 2][:, :], adj_t[T, :, c * CH:(c + 1) * CH]).then_inc(a_in[c % 2], 16)
                    if isinstance(T, int) and T < 3:
                        if T == 0:
                            sp.dma_start(xt[:, :], x_t[0, :, :]).then_inc(x_in, 16)
                        return
                    sp.wait_ge(g_q, (T - 2) * KQ)
                    sp.dma_start(x1_t[T - 3, :, :], x1s[:, :]).then_inc(x_out, 16)
                    if not (isinstance(T, int) and T > NT + 1):
                        sp.dma_start(xt[:, :], x_t[T - 2, :, :]).then_inc(x_in, 16)

                slots(sp, slot, 0, NT + 2)
                sp.wait_ge(x_out, NT * 16)

            @block.vector
            def _(dve):
                def mask(e, u, c):
                    b = c % 2
                    if c == 0:
                        wait(dve, a_tr, (e - 1) * NG)
                        nc.vector.tensor_scalar(scol[:, :], WH[:, e, F:F + 1], 1.0, None, ALU.mult)
                    dve.wait_ge(a_in[b], (e * 2 + c // 2 + 1) * 16)
                    nc.vector.tensor_scalar(A[b][:, :], A[b][:, :], 0.0, -NEG, ALU.is_le, ALU.mult)
                    dve.drain()
                    nc.vector.tensor_tensor_reduce(out=Z[u][:, c * CH:(c + 1) * CH], in0=A[b][:, :],
                                                   in1=DB[:, c * CH:(c + 1) * CH], scale=1.0, scalar=LEAST,
                                                   op0=ALU.add, op1=ALU.max,
                                                   accum_out=mx4[:, c:c + 1]).then_inc(a_v[b], 1)

                def maximum(e, u):
                    wait(dve, a_v[1], (e + 1) * 2)
                    nc.vector.tensor_reduce(mx[:, :], mx4[:, :], AX.X, ALU.max).then_inc(a_max, 1)

                def shift(e):
                    dve.wait_ge(a_ms, e + 1)
                    nc.vector.scalar_tensor_tensor(nm[:, :], mxs[:, :], SLOPE, mxs[:, :], ALU.mult,
                                                   ALU.max).then_inc(a_max, 1)
                    dve.wait_ge(a_max, e * KM + 2)
                    nc.vector.tensor_scalar(nm[:, :], nm[:, :], -1.0, None, ALU.mult).then_inc(a_max, 1)

                def leaky(e, u, c):
                    dve.wait_ge(a_x, e * NC + c + 1)
                    z = Z[u][:, c * CH:(c + 1) * CH]
                    nc.vector.scalar_tensor_tensor(z, z, SLOPE, z, ALU.mult, ALU.max).then_inc(a_l, 1)

                def gru(g, part):
                    def after(n):
                        dve.wait_ge(g_v, g * KV + n)

                    def done(ins):
                        ins.then_inc(g_v, 1)
                    if part == 0:
                        dve.wait_ge(a_p, (g + 1) * NC)
                        done(nc.vector.tensor_reduce(rsum[:, :], rs[g_par[0]][:, :], AX.X, ALU.add))
                        after(1)
                        done(nc.vector.reciprocal(rden[:, :], rsum[:, :]))
                        nc.vector.tensor_scalar(hs[:, :], H[:, g, :], 1.0, None, ALU.mult)
                        after(2)
                        dve.wait_ge(a_mm, (g + 1) * NG)
                        done(nc.vector.tensor_scalar(hp[:, :], ACC[g_par[0]][:, 0:F], rden[:, :], None, ALU.mult))
                    elif part == 1:
                        dve.wait_ge(g_p, g * KP + 2)
                        done(nc.vector.tensor_tensor(gs[:, :], GP[:, :], bias[:, :], ALU.add))
                    elif part == 2:
                        dve.wait_ge(g_a, g * KA + 2)
                        done(nc.vector.tensor_scalar(rz[:, :], rz[:, :], 0.5, 0.5, ALU.mult, ALU.add))
                        after(5)
                        done(nc.vector.tensor_tensor(tmp[:, :], rz[:, 0:F], gs[:, 3 * F:4 * F], ALU.mult))
                        after(6)
                        done(nc.vector.tensor_tensor(tmp[:, :], tmp[:, :], gs[:, 2 * F:3 * F], ALU.add))
                    elif part == 3:
                        dve.wait_ge(g_q, (g + 1) * KQ)
                        done(nc.vector.bn_stats(stat[:, :], x1s[:, :]))
                        dve.drain()
                        done(nc.vector.bn_aggr(mv[:, :], stat[:, :]))
                        after(9)
                        done(nc.vector.tensor_scalar(ve[:, :], mv[:, 1:2], EPS, None, ALU.add))
                    elif part == 4:
                        dve.wait_ge(g_r, g + 1)
                        done(nc.vector.tensor_scalar(hp[:, :], x1s[:, :], mv[:, 0:1], rstd[:, :], ALU.subtract,
                                                     ALU.mult))
                        after(11)
                        done(nc.vector.tensor_scalar(hp[:, :], hp[:, :], 0.0, None, ALU.max))
                    else:
                        dve.wait_ge(g_p, g * KP + 4)
                        done(nc.vector.tensor_tensor(H[:, g, :], GP[:, 0:F], b1b[:, :], ALU.add))

                g_par = [0]
                ORDER = ["v0", "late", "g0", "v1", "v2", "g1", "v3", "max", "g2", "shift", "l0", "l1", "l2", "l3",
                         "g3", "g4"]

                def slot(T, u):
                    has_g = not (isinstance(T, int) and (T < 1 or T > NT))
                    has_e = not (isinstance(T, int) and T > NT - 2)
                    g_par[0] = 1 - u
                    for what in ORDER:
                        if what == "late":
                            if not (isinstance(T, int) and T < 2):
                                gru(T - 2, 5)
                        elif what[0] == "g":
                            if has_g:
                                gru(T - 1, int(what[1]))
                        elif has_e:
                            if what[0] == "v":
                                mask(T + 1, 1 - u, int(what[1]))
                            elif what[0] == "l":
                                leaky(T + 1, 1 - u, int(what[1]))
                            elif what == "max":
                                maximum(T + 1, 1 - u)
                            else:
                                shift(T + 1)

                for T in range(-1, 0):
                    slot(T, 1)
                slots(dve, slot, 0, NT + 1)

            @block.gpsimd
            def _(pool):
                def step(g):
                    def done(ins):
                        ins.then_inc(g_q, 1)
                    pool.wait_ge(g_a, g * KA + 3)
                    done(nc.gpsimd.tensor_tensor(xp[:, :], hs[:, :], nn[:, :], ALU.subtract))
                    pool.wait_ge(g_q, g * KQ + 1)
                    done(nc.gpsimd.tensor_tensor(xp[:, :], xp[:, :], rz[:, F:2 * F], ALU.mult))
                    pool.wait_ge(g_q, g * KQ + 2)
                    done(nc.gpsimd.tensor_tensor(xp[:, :], xp[:, :], nn[:, :], ALU.add))
                    pool.wait_ge(g_q, g * KQ + 3)
                    pool.wait_ge(x_in, (g + 1) * 16)
                    wait(pool, x_out, g * 16)
                    done(nc.gpsimd.tensor_tensor(x1s[:, :], xp[:, :], xt[:, :], ALU.add))
                    pool.wait_ge(g_v, g * KV + 10)
                    nc.gpsimd.tensor_tensor(rstd[:, :], ve[:, :], half[:, :], ALU.pow).then_inc(g_r, 1)

                step(0)
                with pool.Fori(1, NT) as g:
                    step(g)

            @block.scalar
            def _(act):
                def add(e, u, c):
                    act.wait_ge(a_v[c % 2], e * 2 + c // 2 + 1)
                    z = Z[u][:, c * CH:(c + 1) * CH]
                    nc.scalar.activation(z, z, ACT.Identity, bias=scol[:, :]).then_inc(a_x, 1)

                def add_max(e):
                    act.wait_ge(a_max, e * KM + 1)
                    nc.scalar.activation(mxs[:, :], mx[:, :], ACT.Identity, bias=scol[:, :]).then_inc(a_ms, 1)

                def exp(e, u, c):
                    act.wait_ge(a_l, e * NC + c + 1)
                    if c == 0:
                        act.wait_ge(a_max, (e + 1) * KM)
                    z = Z[u][:, c * CH:(c + 1) * CH]
                    nc.scalar.activation(z, z, ACT.Exp, bias=nm[:, :], accum_out=rs[u][:, c:c + 1]).then_inc(a_p, 1)

                def copy(T, c):
                    act.wait_ge(a_tr, T * NG + c + 1)
                    wait(act, a_mm, T * NG + c + 1 - NB)
                    nc.scalar.activation(PT[c % NB][:, :], TP[c % NB][:, :], ACT.Copy).then_inc(a_pt, 1)

                def gru(g, part):
                    if part == 0:
                        act.wait_ge(g_p, g * KP + 1)
                        nc.scalar.activation(gT[:, :], TG[:, 0:2 * F], ACT.Copy).then_inc(g_a, 1)
                    elif part == 1:
                        act.wait_ge(g_v, g * KV + 4)
                        nc.scalar.activation(rz[:, :], gs[:, 0:2 * F], ACT.Tanh, scale=0.5).then_inc(g_a, 1)
                    elif part == 2:
                        act.wait_ge(g_v, g * KV + 7)
                        nc.scalar.activation(nn[:, :], tmp[:, :], ACT.Tanh).then_inc(g_a, 1)
                    else:
                        act.wait_ge(g_p, g * KP + 3)
                        nc.scalar.activation(gT[:, 0:F], TG[:, 0:F], ACT.Copy).then_inc(g_a, 1)

                PLAN = {0: ["late"], 3: ["x0"], 4: ["g0"], 5: ["x1"], 7: ["g1"], 8: ["x2"], 9: ["m", "x3"], 10: ["g2"],
                        12: ["e0"], 13: ["e1"], 15: ["e2", "e3"]}

                def slot(T, u):
                    has_t = not (isinstance(T, int) and (T < 0 or T > NT - 1))
                    has_g = not (isinstance(T, int) and (T < 1 or T > NT))
                    has_e = not (isinstance(T, int) and T > NT - 2)
                    for c in range(NG):
                        if has_t:
                            copy(T, c)
                        for what in PLAN.get(c, []):
                            if what == "late":
                                if not (isinstance(T, int) and T < 2):
                                    gru(T - 2, 3)
                            elif what[0] == "g" and has_g:
                                gru(T - 1, int(what[1]))
                            elif what == "m" and has_e:
                                add_max(T + 1)
                            elif what[0] == "x" and has_e:
                                add(T + 1, 1 - u, int(what[1]))
                            elif what[0] == "e" and has_e:
                                exp(T + 1, 1 - u, int(what[1]))

                slot(-1, 1)
                slots(act, slot, 0, NT + 1)

            @block.tensor
            def _(pe):
                def transposes(T, u, c):
                    if c % GPC == 0:
                        pe.wait_ge(a_p, T * NC + c // GPC + 1)
                    wait(pe, a_pt, T * NG + c + 1 - NB)
                    for k in range(4):
                        j = 4 * c + k
                        ins = nc.tensor.transpose(TP[c % NB][:, k * P:(k + 1) * P], Z[u][:, j * P:(j + 1) * P],
                                                  ident[:, :])
                    ins.then_inc(a_tr, 1)

                def product(T, u, c):
                    if c == 0 and not (isinstance(T, int) and T < 2):
                        pe.wait_ge(g_v, (T - 2) * KV + 3)
                    pe.wait_ge(a_pt, T * NG + c + 1)
                    for k in range(4):
                        j = 4 * c + k
                        ins = nc.tensor.matmul(ACC[u][:, 0:F], PT[c % NB][:, k * P:(k + 1) * P], WH[:, j, 0:F],
                                               start=(j == 0), stop=(j == NT - 1))
                    ins.then_inc(a_mm, 1)

                def gru(g, part):
                    if part == 0:
                        pe.wait_ge(g_v, g * KV + 3)
                        nc.tensor.transpose(TG[:, 0:F], hp[:, :], ident[:, :])
                        nc.tensor.transpose(TG[:, F:2 * F], hs[:, :], ident[:, :]).then_inc(g_p, 1)
                    elif part == 1:
                        pe.wait_ge(g_a, g * KA + 1)
                        nc.tensor.matmul(GP[:, 0:3 * F], gT[:, 0:F], wihT[:, :], start=True, stop=False)
                        nc.tensor.matmul(GP[:, 0:2 * F], gT[:, F:2 * F], whhT[:, 0:2 * F], start=False, stop=False)
                        nc.tensor.matmul(GP[:, 3 * F:4 * F], gT[:, F:2 * F], whhT[:, 2 * F:3 * F], start=False,
                                         stop=True).then_inc(g_p, 1)
                    elif part == 2:
                        pe.wait_ge(g_v, g * KV + 12)
                        nc.tensor.transpose(TG[:, 0:F], hp[:, :], ident[:, :]).then_inc(g_p, 1)
                    else:
                        pe.wait_ge(g_a, g * KA + 4)
                        nc.tensor.matmul(GP[:, 0:F], gT[:, 0:F], w1T[:, :], start=True, stop=True).then_inc(g_p, 1)

                PLAN = {0: (2, 2), 1: (2, 3), 3: (1, 0), 5: (1, 1)}

                def slot(T, u):
                    has_t = not (isinstance(T, int) and T > NT - 1)
                    for c in range(NG):
                        if has_t:
                            transposes(T, u, c)
                            if c >= LAG:
                                product(T, u, c - LAG)
                        if c in PLAN:
                            back, part = PLAN[c]
                            if not isinstance(T, int) or 0 <= T - back < NT:
                                gru(T - back, part)
                    if has_t:
                        for c in range(NG - LAG, NG):
                            product(T, u, c)

                slots(pe, slot, 0, NT + 1)

        l_in, l_x = [sem(f"l_in{b}") for b in range(2)], [sem(f"l_x{b}") for b in range(2)]
        l_tr, l_pt, l_mm, l_o = sem("l_tr"), sem("l_pt"), sem("l_mm"), sem("l_o")
        l_out = [sem(f"l_out{b}") for b in range(2)]
        OB = [OP, GP]
        xin = [gs[:, 0:F], gs[:, F:2 * F]]
        ot = [gs[:, 2 * F:3 * F], gs[:, 3 * F:4 * F]]
        with nc.Block() as block:
            def pairs(eng, slot):
                for T in range(2):
                    slot(T, T, 0)
                with eng.Fori(1, NT // 2) as k:
                    for d in range(2):
                        slot(k * 2 + d, d, k)

            @block.sync
            def _(sp):
                def slot(T, u, n):
                    wait(sp, l_tr, (T - 1) * NG)
                    sp.dma_start(Z[u][:, :], adj_t[T, :, :], max_dma_last_dim=8192).then_inc(l_in[u], 16)
                    wait(sp, l_o, T - 1)
                    sp.dma_start(xin[u], x1_t[T, :, :]).then_inc(l_x[u], 16)

                pairs(sp, slot)

            @block.tensor
            def _(pe):
                def slot(T, u, n):
                    def product(c):
                        pe.wait_ge(l_pt, T * NG + c + 1)
                        if c == 0:
                            wait(pe, l_o, T - 1)
                        for k in range(4):
                            j = 4 * c + k
                            ins = nc.tensor.matmul(OB[u][:, 0:F], PT[c % NB][:, k * P:(k + 1) * P], H[:, j, :],
                                                   start=(j == 0), stop=(j == NT - 1))
                        ins.then_inc(l_mm, 1)

                    for c in range(NG):
                        if c == 0:
                            pe.wait_ge(l_in[u], (n + 1) * 16)
                        wait(pe, l_pt, T * NG + c + 1 - NB)
                        for k in range(4):
                            j = 4 * c + k
                            ins = nc.tensor.transpose(TP[c % NB][:, k * P:(k + 1) * P], Z[u][:, j * P:(j + 1) * P],
                                                      ident[:, :])
                        ins.then_inc(l_tr, 1)
                        if c >= LAG:
                            product(c - LAG)
                    for c in range(NG - LAG, NG):
                        product(c)

                pairs(pe, slot)

            @block.scalar
            def _(act):
                def slot(T, u, n):
                    for c in range(NG):
                        act.wait_ge(l_tr, T * NG + c + 1)
                        wait(act, l_mm, T * NG + c + 1 - NB)
                        nc.scalar.activation(PT[c % NB][:, :], TP[c % NB][:, :], ACT.Copy).then_inc(l_pt, 1)

                pairs(act, slot)

            @block.vector
            def _(dve):
                def slot(T, u, n):
                    dve.wait_ge(l_mm, (T + 1) * NG)
                    dve.wait_ge(l_x[u], (n + 1) * 16)
                    wait(dve, l_out[u], n * 16)
                    nc.vector.tensor_tensor(ot[u], OB[u][:, 0:F], xin[u], ALU.add).then_inc(l_o, 1)

                pairs(dve, slot)

            @block.gpsimd
            def _(pool):
                def slot(T, u, n):
                    pool.wait_ge(l_o, T + 1)
                    pool.dma_start(out_t[T, :, :], ot[u]).then_inc(l_out[u], 16)

                pairs(pool, slot)
                for b in range(2):
                    pool.wait_ge(l_out[b], NT // 2 * 16)


_INS = ['x', 'adj', 'L0_gnn_W', 'L0_gnn_a', 'L0_gnn_w_ih', 'L0_gnn_w_hh', 'L0_gnn_b_ih', 'L0_gnn_b_hh',
        'L1_gnn_W', 'L1_gnn_b']
_OUTS = [((8192, 128), 'float32')]


def kernel(**inputs):
    import numpy as _np
    import concourse.bacc as _bacc
    from concourse import mybir as _mybir
    from concourse.bass_utils import run_bass_kernel_spmd as _run

    nc = _bacc.Bacc("TRN2", target_bir_lowering=False, num_devices=1)
    arrays, args = {}, []
    for name in _INS:
        arr = _np.ascontiguousarray(inputs[name])
        arrays[f"in_{name}_dram"] = arr
        args.append(nc.dram_tensor(f"in_{name}_dram", arr.shape, _mybir.dt.from_np(arr.dtype),
                                   kind="ExternalInput").ap())
    for i, (shape, dtype) in enumerate(_OUTS):
        dt = _mybir.dt.from_np(_np.dtype(dtype))
        args.append(nc.dram_tensor(f"out_{i}_dram", shape, dt, kind="ExternalOutput").ap())
    graph_layers(nc, *args)
    r = _run(nc, [arrays], core_ids=[0])
    return r.results[0]["out_0_dram"]
```

```python
from contextlib import ExitStack

import concourse.bass as bass
from concourse import mybir

N = 8192
F = 128
P = 128
NT = N // P
CH = 2048
NC = N // CH
GC = 512
NG = N // GC
GPC = CH // GC
NB = 4
LAG = 2
POOLED = (0, 3)
CREDIT = 1
SLOPE = 0.2
NEG = 9000000000000000.0
GSCALE = 128.0
GMOST = 256.0
GLEAST = 2.0 ** -6
LEAST = -3.0e38
EPS = 1e-5

f32 = mybir.dt.float32
f16 = mybir.dt.float16
ALU = mybir.AluOpType
ACT = mybir.ActivationFunctionType
AX = mybir.AxisListType


def graph_layers(nc, x, adj, w, a, w_ih, w_hh, b_ih, b_hh, w1, b1, out):
    x_t = x.rearrange("(t p) f -> t p f", p=P)
    out_t = out.rearrange("(t p) f -> t p f", p=P)
    adj_t = adj.rearrange("(t p) n -> t p n", p=P)

    ctx = ExitStack()
    with ctx:
        def sb(name, shape, dt=f32):
            return ctx.enter_context(nc.sbuf_tensor(name, shape, dt))

        def ps(name):
            return ctx.enter_context(nc.psum_tensor(name, [P, 512], f32))

        def sem(name):
            return ctx.enter_context(nc.semaphore(name))

        H = sb("H", [P, NT, F])
        WH = sb("WH", [P, NT, F + 2])
        DB = sb("DB", [P, N])
        Z = [sb(f"Z{b}", [P, N]) for b in range(2)]
        PT = [sb(f"PT{b}", [P, GC]) for b in range(NB)]
        ident = sb("ident", [P, P])
        ones = sb("ones", [1, P])
        wext = sb("wext", [P, F + 2])
        wab = sb("wab", [P, P])
        wT = sb("wT", [P, F])
        w1T = sb("w1T", [P, F])
        acol = sb("acol", [P, 2])
        wihT = sb("wihT", [P, 3 * F])
        whhT = sb("whhT", [P, 3 * F])
        raw = Z[0][:, 0:7 * F].rearrange("p (c f) -> p c f", f=F)
        brow = Z[1][0:1, 0:7 * F]
        bsum = Z[1][0:1, 7 * F:9 * F]
        bias = sb("bias", [P, 4 * F])
        b1b = sb("b1b", [P, F])
        epst = sb("epst", [P, 1])
        stat = sb("stat", [P, 6])
        mv = sb("mv", [P, 2])
        rstd = sb("rstd", [P, 1])
        hs = sb("hs", [P, F])
        xt = sb("xt", [P, F])
        hp = sb("hp", [P, F])
        gT = sb("gT", [P, 2 * F])
        gs = sb("gs", [P, 4 * F])
        rz = sb("rz", [P, 2 * F])
        nn = sb("nn", [P, F])
        tmp = sb("tmp", [P, F])
        x1s = sb("x1s", [P, F])
        xp = sb("xp", [P, F])
        ve = sb("ve", [P, 1])
        step_v, step_p = sb("step_v", [P, 2 * NC]), sb("step_p", [P, 2 * NC])
        half = sb("half", [P, 1])
        scol = sb("scol", [P, 1])
        mx4 = sb("mx4", [P, NC])
        mx = sb("mx", [P, 1])
        mxs = sb("mxs", [P, 1])
        nm = sb("nm", [P, 1])
        rs = [sb(f"rs{b}", [P, NC]) for b in range(2)]
        rsum = sb("rsum", [P, 1])
        rden = sb("rden", [P, 1])
        x1_dram = nc.dram_tensor("x_after_layer_0", [N, F], f32)
        x1_t = x1_dram.ap().rearrange("(t p) f -> t p f", p=P)

        TP = [ps(f"TP{b}") for b in range(NB)]
        TG = ps("TG")
        GP = ps("GP")
        OP = ps("OP")
        OQ = ps("OQ")
        ACC = [OP, OQ]

        s_in, s_id, s_tr, s_cp, s_v = (sem(n) for n in ("w_in", "w_id", "w_tr", "w_cp", "w_v"))
        with nc.Block() as block:
            @block.sync
            def _(sp):
                sp.dma_start(H[:, :, :], x.rearrange("(t p) f -> p t f", p=P)).then_inc(s_in, 16)
                sp.dma_start(raw[:, 0, :], w).then_inc(s_in, 16)
                sp.dma_start(raw[:, 1:4, :], w_ih.rearrange("(c p) f -> p c f", p=P)).then_inc(s_in, 16)
                sp.dma_start(raw[:, 4:7, :], w_hh.rearrange("(c p) f -> p c f", p=P)).then_inc(s_in, 16)
                sp.dma_start(w1T[:, :], w1).then_inc(s_in, 16)
                for c in range(2):
                    sp.dma_start(acol[:, c:c + 1], a[c * F:(c + 1) * F, :]).then_inc(s_in, 16)
                sp.dma_start(brow[0:1, 0:3 * F], b_ih.rearrange("(o n) -> o n", o=1)).then_inc(s_in, 16)
                sp.dma_start(brow[0:1, 3 * F:6 * F], b_hh.rearrange("(o n) -> o n", o=1)).then_inc(s_in, 16)
                sp.dma_start(brow[0:1, 6 * F:7 * F], b1.rearrange("(o n) -> o n", o=1)).then_inc(s_in, 16)

            @block.gpsimd
            def _(pool):
                nc.gpsimd.memset(ident[:, :], 0.0).then_inc(s_id, 1)
                nc.gpsimd.memset(ones[:, :], 1.0).then_inc(s_id, 1)
                nc.gpsimd.memset(epst[:, :], EPS).then_inc(s_id, 1)
                nc.gpsimd.memset(half[:, :], -0.5).then_inc(s_id, 1)
                pool.wait_ge(s_id, 4)
                nc.gpsimd.affine_select(out=ident[:, :], in_=ident[:, :], compare_op=ALU.not_equal, fill=1.0,
                                        base=0, pattern=[[-1, P]], channel_multiplier=1).then_inc(s_id, 1)

            @block.tensor
            def _(pe):
                pe.wait_ge(s_in, 160)
                pe.wait_ge(s_id, 5)
                for k in range(8):
                    src = raw[:, k, :] if k < 7 else w1T[:, :]
                    bank = (TP[0], TP[1])[k // 4]
                    ins = nc.tensor.transpose(bank[:, (k % 4) * F:(k % 4 + 1) * F], src, ident[:, :])
                ins.then_inc(s_tr, 1)
                pe.wait_ge(s_cp, 4)
                nc.tensor.matmul(TG[:, 0:2], wT[:, :], acol[:, :], start=True, stop=True).then_inc(s_tr, 1)
                pe.wait_ge(s_v, 1)
                nc.tensor.matmul(GP[:, 0:2 * F], ones[:, :], bsum[0:1, :], start=True, stop=True)
                nc.tensor.matmul(GP[:, 2 * F:3 * F], ones[:, :], brow[0:1, 2 * F:3 * F], start=True, stop=True)
                nc.tensor.matmul(GP[:, 3 * F:4 * F], ones[:, :], brow[0:1, 5 * F:6 * F], start=True, stop=True)
                nc.tensor.matmul(OP[:, 0:F], ones[:, :], brow[0:1, 6 * F:7 * F], start=True,
                                 stop=True).then_inc(s_tr, 1)

            @block.vector
            def _(dve):
                dve.wait_ge(s_in, 160)
                nc.vector.tensor_tensor(bsum[0:1, :], brow[0:1, 0:2 * F], brow[0:1, 3 * F:5 * F], ALU.add).then_inc(s_v, 1)
                dve.wait_ge(s_tr, 1)
                nc.vector.tensor_copy(wT[:, :], TP[0][:, 0:F]).then_inc(s_cp, 1)
                nc.vector.tensor_copy(wihT[:, :], TP[0][:, F:4 * F]).then_inc(s_cp, 1)
                nc.vector.tensor_copy(whhT[:, :], TP[1][:, 0:3 * F]).then_inc(s_cp, 1)
                nc.vector.tensor_copy(w1T[:, :], TP[1][:, 3 * F:4 * F]).then_inc(s_cp, 1)
                nc.vector.tensor_copy(wext[:, 0:F], raw[:, 0, :]).then_inc(s_v, 1)
                dve.wait_ge(s_tr, 2)
                nc.vector.tensor_copy(wext[:, F:F + 2], TG[:, 0:2]).then_inc(s_v, 1)
                nc.vector.tensor_copy(wab[:, :], TG[:, 1:2].to_broadcast([P, P])).then_inc(s_v, 1)
                dve.wait_ge(s_tr, 3)
                nc.vector.tensor_copy(bias[:, :], GP[:, :]).then_inc(s_v, 1)
                nc.vector.tensor_copy(b1b[:, :], OP[:, 0:F]).then_inc(s_v, 1)

        n_dve, n_std, n_hs, n_tr, n_hT, n_mm, n_wh, n_db = (
            sem(n) for n in ("n_dve", "n_std", "n_hs", "n_tr", "n_hT", "n_mm", "n_wh", "n_db"))
        B = 4
        hb = Z[0][:, 0:B * F]
        hbT = Z[1][:, 0:B * F]
        stb = Z[0][:, 1024:1024 + B * 6].rearrange("p (b k) -> p b k", k=6)
        mvb = Z[0][:, 1088:1088 + B * 2].rearrange("p (b k) -> p b k", k=2)
        sdb = Z[0][:, 1120:1120 + B]
        rsb = Z[0][:, 1152:1152 + B]
        with nc.Block() as block:
            @block.vector
            def _(dve):
                dve.sem_inc(n_dve, CREDIT)
                with dve.Fori(0, NT // B) as k:
                    for b in range(B):
                        nc.vector.bn_stats(stb[:, b, :], H[:, k * B + b, :])
                    dve.drain()
                    for b in range(B):
                        nc.vector.bn_aggr(mvb[:, b, :], stb[:, b, :]).then_inc(n_dve, 1)
                    dve.wait_ge(n_std, k + 1)
                    nc.vector.reciprocal(rsb, sdb).then_inc(n_dve, 1)
                    dve.wait_ge(n_dve, CREDIT + k * 6 + 5)
                    dve.wait_ge(n_tr, CREDIT + k)
                    for b in range(B):
                        ins = nc.vector.tensor_scalar(hb[:, b * F:(b + 1) * F], H[:, k * B + b, :], mvb[:, b, 0:1],
                                                      rsb[:, b:b + 1], ALU.subtract, ALU.mult)
                    ins.then_inc(n_dve, 1)
                    dve.wait_ge(n_dve, CREDIT + k * 6 + 6)
                    nc.vector.tensor_scalar(hb, hb, 0.0, None, ALU.max).then_inc(n_hs, 1)
                    dve.wait_ge(n_hs, k + 1)
                    nc.vector.tensor_scalar(H[:, bass.ts(k, B), :].rearrange("p b f -> p (b f)"), hb, 1.0, None,
                                            ALU.mult)
                    dve.wait_ge(n_mm, CREDIT + k + 1)
                    for half_ in range(2):
                        ins = nc.vector.tensor_scalar(
                            WH[:, bass.ds(k * B + half_ * 2, 2), :].rearrange("p b f -> p (b f)"),
                            (GP, OP)[half_][:, 0:2 * (F + 2)], 1.0, None, ALU.mult)
                    ins.then_inc(n_wh, 1)

            @block.scalar
            def _(act):
                act.sem_inc(n_hT, CREDIT)
                with act.Fori(0, NT // B) as k:
                    act.wait_ge(n_dve, CREDIT + k * 6 + 4)
                    nc.scalar.activation(sdb, mvb[:, :, 1:2].rearrange("p b k -> p (b k)"), ACT.Sqrt,
                                         bias=epst[:, :]).then_inc(n_std, 1)
                    act.wait_ge(n_tr, CREDIT + k + 1)
                    act.wait_ge(n_mm, CREDIT + k)
                    nc.scalar.activation(hbT, TG[:, :], ACT.Copy).then_inc(n_hT, 1)
                    act.wait_ge(n_mm, CREDIT + k + 1)
                    nc.scalar.activation(DB[:, bass.ts(k, B * P)], OQ[:, :], ACT.Copy).then_inc(n_db, 1)

            @block.tensor
            def _(pe):
                pe.sem_inc(n_tr, CREDIT)
                pe.sem_inc(n_mm, CREDIT)
                pe.sem_inc(n_wh, CREDIT)
                pe.sem_inc(n_db, CREDIT)
                with pe.Fori(0, NT // B) as k:
                    pe.wait_ge(n_hs, k + 1)
                    pe.wait_ge(n_hT, CREDIT + k)
                    for b in range(B):
                        ins = nc.tensor.transpose(TG[:, b * F:(b + 1) * F], hb[:, b * F:(b + 1) * F], ident[:, :])
                    ins.then_inc(n_tr, 1)
                    pe.wait_ge(n_hT, CREDIT + k + 1)
                    pe.wait_ge(n_wh, CREDIT + k)
                    pe.wait_ge(n_db, CREDIT + k)
                    for b in range(B):
                        at = (b % 2) * (F + 2)
                        nc.tensor.matmul((GP, OP)[b // 2][:, at:at + F + 2], hbT[:, b * F:(b + 1) * F], wext[:, :],
                                         start=True, stop=True)
                    nc.tensor.matmul(OQ[:, :], wab[:, :], hbT, start=True, stop=True).then_inc(n_mm, 1)

        a_in = [[sem(f"a_in{b}{c}") for c in range(NC)] for b in range(2)]
        a_k = sem("a_k")
        a_v = sem("a_v")
        a_max = sem("a_max")
        a_ms = sem("a_ms")
        a_x = sem("a_x")
        a_l = sem("a_l")
        a_p = sem("a_p")
        a_tr = sem("a_tr")
        a_pt = sem("a_pt")
        a_mm = sem("a_mm")
        g_v, g_a, g_p, g_r = sem("g_v"), sem("g_a"), sem("g_p"), sem("g_r")
        g_q = sem("g_q")
        x_in, x_out = sem("x_in"), sem("x_out")
        KM, KV, KA, KP, KQ = 3, 13, 4, 4, 4

        def wait(eng, s, value):
            if not isinstance(value, int) or value > 0:
                eng.wait_ge(s, value)

        def slots(eng, slot, first, last):
            for T in range(first, 3):
                slot(T, T % 2, T // 2)
            with eng.Fori(0, (NT - 4) // 2) as k:
                for d in range(3, 5):
                    slot(k * 2 + d, d % 2, k + d // 2)
            for T in range(NT - 1, last + 1):
                slot(T, T % 2, T // 2)

        with nc.Block() as block:
            @block.sync
            def _(sp):
                def x_store(g):
                    sp.wait_ge(g_q, (g + 1) * KQ)
                    sp.dma_start(x1_t[g, :, :], x1s[:, :]).then_inc(x_out, 16)

                def slot(T, u, n):
                    if not (isinstance(T, int) and T < 3):
                        x_store(T - 3)
                    if not isinstance(T, int) or 3 <= T <= NT + 1:
                        sp.dma_start(xt[:, :], x_t[T - 2, :, :]).then_inc(x_in, 16)
                    if isinstance(T, int) and T > NT - 2:
                        return
                    for c in range(NC):
                        wait(sp, a_tr, (T - 1) * NG + (c + 1) * GPC)
                        sp.dma_start(Z[1 - u][:, c * CH:(c + 1) * CH],
                                     adj_t[T + 1, :, c * CH:(c + 1) * CH]).then_inc(a_in[1 - u][c], 16)

                slot(-1, 1, -1)
                sp.dma_start(xt[:, :], x_t[0, :, :]).then_inc(x_in, 16)
                slots(sp, slot, 0, NT + 2)
                sp.wait_ge(x_out, NT * 16)

            @block.vector
            def _(dve):
                def mask(e, u, m, c):
                    z = Z[u][:, c * CH:(c + 1) * CH]
                    if c == 0:
                        nc.vector.tensor_scalar(scol[:, :], WH[:, e, F:F + 1], 1.0, None, ALU.mult)
                    if c in POOLED:
                        dve.wait_ge(a_k, e * len(POOLED) + POOLED.index(c) + 1)
                        nc.vector.tensor_scalar(step_v[:, u * NC + c:u * NC + c + 1], half[:, :], 1.0, None, ALU.mult)
                    else:
                        dve.wait_ge(a_in[u][c], (m + 1) * 16)
                        nc.vector.tensor_scalar(z, z, 0.0, -NEG, ALU.is_le, ALU.mult)
                        dve.drain()
                    nc.vector.tensor_tensor_reduce(out=z, in0=z, in1=DB[:, c * CH:(c + 1) * CH], scale=1.0,
                                                   scalar=LEAST, op0=ALU.add, op1=ALU.max,
                                                   accum_out=mx4[:, c:c + 1]).then_inc(a_v, 1)

                def maximum(e, u):
                    wait(dve, a_v, (e + 1) * NC)
                    nc.vector.tensor_reduce(mx[:, :], mx4[:, :], AX.X, ALU.max).then_inc(a_max, 1)

                def shift(e):
                    dve.wait_ge(a_ms, e + 1)
                    nc.vector.scalar_tensor_tensor(nm[:, :], mxs[:, :], SLOPE, mxs[:, :], ALU.mult,
                                                   ALU.max).then_inc(a_max, 1)
                    dve.wait_ge(a_max, e * KM + 2)
                    nc.vector.tensor_scalar(nm[:, :], nm[:, :], -1.0, None, ALU.mult).then_inc(a_max, 1)

                def leaky(e, u, c):
                    dve.wait_ge(a_x, e * NC + c + 1)
                    z = Z[u][:, c * CH:(c + 1) * CH]
                    nc.vector.scalar_tensor_tensor(z, z, SLOPE, z, ALU.mult, ALU.max).then_inc(a_l, 1)

                def gru(g, part):
                    def after(n):
                        dve.wait_ge(g_v, g * KV + n)

                    def done(ins):
                        ins.then_inc(g_v, 1)
                    if part == 0:
                        dve.wait_ge(a_p, (g + 1) * NC)
                        done(nc.vector.tensor_reduce(rsum[:, :], rs[g_par[0]][:, :], AX.X, ALU.add))
                        after(1)
                        done(nc.vector.reciprocal(rden[:, :], rsum[:, :]))
                        nc.vector.tensor_scalar(hs[:, :], H[:, g, :], 1.0, None, ALU.mult)
                        after(2)
                        dve.wait_ge(a_mm, (g + 1) * NG)
                        done(nc.vector.tensor_scalar(hp[:, :], ACC[g_par[0]][:, 0:F], rden[:, :], None, ALU.mult))
                    elif part == 1:
                        dve.wait_ge(g_p, g * KP + 2)
                        done(nc.vector.tensor_tensor(gs[:, :], GP[:, :], bias[:, :], ALU.add))
                    elif part == 2:
                        dve.wait_ge(g_a, g * KA + 2)
                        done(nc.vector.tensor_scalar(rz[:, :], rz[:, :], 0.5, 0.5, ALU.mult, ALU.add))
                        after(5)
                        done(nc.vector.tensor_tensor(tmp[:, :], rz[:, 0:F], gs[:, 3 * F:4 * F], ALU.mult))
                        after(6)
                        done(nc.vector.tensor_tensor(tmp[:, :], tmp[:, :], gs[:, 2 * F:3 * F], ALU.add))
                    elif part == 3:
                        dve.wait_ge(g_q, (g + 1) * KQ)
                        done(nc.vector.bn_stats(stat[:, :], x1s[:, :]))
                        dve.drain()
                        done(nc.vector.bn_aggr(mv[:, :], stat[:, :]))
                        after(9)
                        done(nc.vector.tensor_scalar(ve[:, :], mv[:, 1:2], EPS, None, ALU.add))
                    elif part == 4:
                        dve.wait_ge(g_r, g + 1)
                        done(nc.vector.tensor_scalar(hp[:, :], x1s[:, :], mv[:, 0:1], rstd[:, :], ALU.subtract,
                                                     ALU.mult))
                        after(11)
                        done(nc.vector.tensor_scalar(hp[:, :], hp[:, :], 0.0, None, ALU.max))
                    else:
                        dve.wait_ge(g_p, g * KP + 4)
                        done(nc.vector.tensor_tensor(H[:, g, :], GP[:, 0:F], b1b[:, :], ALU.add))

                g_par = [0]
                ORDER = ["v0", "root", "v1", "late", "g0", "v2", "l0", "g1", "v3", "max", "l1", "shift", "g2", "l2", "l3",
                         "g3"]

                def slot(T, u, n):
                    has_g = not (isinstance(T, int) and (T < 1 or T > NT))
                    has_e = not (isinstance(T, int) and T > NT - 2)
                    g_par[0] = 1 - u
                    for what in ORDER:
                        if what in ("root", "late"):
                            if not (isinstance(T, int) and T < 2):
                                gru(T - 2, 4 if what == "root" else 5)
                        elif what[0] == "g":
                            if has_g:
                                gru(T - 1, int(what[1]))
                        elif has_e:
                            if what[0] == "v":
                                mask(T + 1, 1 - u, n + u, int(what[1]))
                            elif what[0] == "l":
                                leaky(T + 1, 1 - u, int(what[1]))
                            elif what == "max":
                                maximum(T + 1, 1 - u)
                            else:
                                shift(T + 1)

                for T in range(-1, 0):
                    slot(T, 1, -1)
                slots(dve, slot, 0, NT + 1)

            @block.gpsimd
            def _(pool):
                def step(g):
                    def done(ins):
                        ins.then_inc(g_q, 1)
                    pool.wait_ge(g_a, g * KA + 3)
                    done(nc.gpsimd.tensor_tensor(xp[:, :], hs[:, :], nn[:, :], ALU.subtract))
                    pool.wait_ge(g_q, g * KQ + 1)
                    done(nc.gpsimd.tensor_tensor(xp[:, :], xp[:, :], rz[:, F:2 * F], ALU.mult))
                    pool.wait_ge(g_q, g * KQ + 2)
                    done(nc.gpsimd.tensor_tensor(xp[:, :], xp[:, :], nn[:, :], ALU.add))
                    pool.wait_ge(g_q, g * KQ + 3)
                    pool.wait_ge(x_in, (g + 1) * 16)
                    wait(pool, x_out, g * 16)
                    done(nc.gpsimd.tensor_tensor(x1s[:, :], xp[:, :], xt[:, :], ALU.add))
                    pool.wait_ge(g_v, g * KV + 10)
                    nc.gpsimd.tensor_tensor(rstd[:, :], ve[:, :], half[:, :], ALU.pow).then_inc(g_r, 1)

                def mask(e, u, m, c):
                    pool.wait_ge(a_in[u][c], (m + 1) * 16)
                    nc.gpsimd.tensor_tensor(step_p[:, u * NC + c:u * NC + c + 1], half[:, :], half[:, :], ALU.add)
                    z = Z[u][:, c * CH:(c + 1) * CH]
                    nc.gpsimd.tensor_scalar(z, z, 0.0, -NEG, ALU.is_le, ALU.mult).then_inc(a_k, 1)

                def slot(T, u, n):
                    for what in ORDER:
                        if what == "g":
                            if not isinstance(T, int) or 2 <= T:
                                step(T - 2)
                        elif not (isinstance(T, int) and T > NT - 2):
                            mask(T + 1, 1 - u, n + u, int(what[1]))

                ORDER = ["k0", "g", "k3"]
                slot(-1, 1, -1)
                slots(pool, slot, 0, NT + 1)

            @block.scalar
            def _(act):
                def add(e, u, c):
                    act.wait_ge(a_v, e * NC + c + 1)
                    z = Z[u][:, c * CH:(c + 1) * CH]
                    nc.scalar.activation(z, z, ACT.Identity, bias=scol[:, :]).then_inc(a_x, 1)

                def add_max(e):
                    act.wait_ge(a_max, e * KM + 1)
                    nc.scalar.activation(mxs[:, :], mx[:, :], ACT.Identity, bias=scol[:, :]).then_inc(a_ms, 1)

                def exp(e, u, c):
                    act.wait_ge(a_l, e * NC + c + 1)
                    if c == 0:
                        act.wait_ge(a_max, (e + 1) * KM)
                    z = Z[u][:, c * CH:(c + 1) * CH]
                    nc.scalar.activation(z, z, ACT.Exp, bias=nm[:, :], accum_out=rs[u][:, c:c + 1]).then_inc(a_p, 1)

                def copy(T, c):
                    act.wait_ge(a_tr, T * NG + c + 1)
                    wait(act, a_mm, T * NG + c + 1 - NB)
                    nc.scalar.activation(PT[c % NB][:, :], TP[c % NB][:, :], ACT.Copy).then_inc(a_pt, 1)

                def gru(g, part):
                    if part == 0:
                        act.wait_ge(g_p, g * KP + 1)
                        nc.scalar.activation(gT[:, :], TG[:, 0:2 * F], ACT.Copy).then_inc(g_a, 1)
                    elif part == 1:
                        act.wait_ge(g_v, g * KV + 4)
                        nc.scalar.activation(rz[:, :], gs[:, 0:2 * F], ACT.Tanh, scale=0.5).then_inc(g_a, 1)
                    elif part == 2:
                        act.wait_ge(g_v, g * KV + 7)
                        nc.scalar.activation(nn[:, :], tmp[:, :], ACT.Tanh).then_inc(g_a, 1)
                    else:
                        act.wait_ge(g_p, g * KP + 3)
                        nc.scalar.activation(gT[:, 0:F], TG[:, 0:F], ACT.Copy).then_inc(g_a, 1)

                PLAN = {0: ["f2"], 1: ["late"], 2: ["f3"], 4: ["g0", "x0"], 5: ["x1"], 7: ["x2"], 8: ["g1"], 10: ["m", "x3"],
                        11: ["g2"], 13: ["e0"], 15: ["e1"]}

                def slot(T, u, n):
                    has_t = not (isinstance(T, int) and (T < 0 or T > NT - 1))
                    has_g = not (isinstance(T, int) and (T < 1 or T > NT))
                    has_e = not (isinstance(T, int) and T > NT - 2)
                    for c in range(NG):
                        if has_t:
                            copy(T, c)
                        for what in PLAN.get(c, []):
                            if what == "late":
                                if not (isinstance(T, int) and T < 2):
                                    gru(T - 2, 3)
                            elif what[0] == "g" and has_g:
                                gru(T - 1, int(what[1]))
                            elif what[0] == "f" and has_t:
                                exp(T, u, int(what[1]))
                            elif what == "m" and has_e:
                                add_max(T + 1)
                            elif what[0] == "x" and has_e:
                                add(T + 1, 1 - u, int(what[1]))
                            elif what[0] == "e" and has_e:
                                exp(T + 1, 1 - u, int(what[1]))

                slot(-1, 1, -1)
                slots(act, slot, 0, NT + 1)

            @block.tensor
            def _(pe):
                def transposes(T, u, c):
                    if c % GPC == 0:
                        pe.wait_ge(a_p, T * NC + c // GPC + 1)
                    wait(pe, a_pt, T * NG + c + 1 - NB)
                    for k in range(4):
                        j = 4 * c + k
                        ins = nc.tensor.transpose(TP[c % NB][:, k * P:(k + 1) * P], Z[u][:, j * P:(j + 1) * P],
                                                  ident[:, :])
                    ins.then_inc(a_tr, 1)

                def product(T, u, c):
                    if c == 0 and not (isinstance(T, int) and T < 2):
                        pe.wait_ge(g_v, (T - 2) * KV + 3)
                    pe.wait_ge(a_pt, T * NG + c + 1)
                    for k in range(4):
                        j = 4 * c + k
                        ins = nc.tensor.matmul(ACC[u][:, 0:F], PT[c % NB][:, k * P:(k + 1) * P], WH[:, j, 0:F],
                                               start=(j == 0), stop=(j == NT - 1))
                    ins.then_inc(a_mm, 1)

                def gru(g, part):
                    if part == 0:
                        pe.wait_ge(g_v, g * KV + 3)
                        nc.tensor.transpose(TG[:, 0:F], hp[:, :], ident[:, :])
                        nc.tensor.transpose(TG[:, F:2 * F], hs[:, :], ident[:, :]).then_inc(g_p, 1)
                    elif part == 1:
                        pe.wait_ge(g_a, g * KA + 1)
                        nc.tensor.matmul(GP[:, 0:3 * F], gT[:, 0:F], wihT[:, :], start=True, stop=False)
                        nc.tensor.matmul(GP[:, 0:2 * F], gT[:, F:2 * F], whhT[:, 0:2 * F], start=False, stop=False)
                        nc.tensor.matmul(GP[:, 3 * F:4 * F], gT[:, F:2 * F], whhT[:, 2 * F:3 * F], start=False,
                                         stop=True).then_inc(g_p, 1)
                    elif part == 2:
                        pe.wait_ge(g_v, g * KV + 12)
                        nc.tensor.transpose(TG[:, 0:F], hp[:, :], ident[:, :]).then_inc(g_p, 1)
                    else:
                        pe.wait_ge(g_a, g * KA + 4)
                        nc.tensor.matmul(GP[:, 0:F], gT[:, 0:F], w1T[:, :], start=True, stop=True).then_inc(g_p, 1)

                PLAN = {0: (2, 2), 2: (2, 3), 4: (1, 0), 6: (1, 1)}

                def slot(T, u, n):
                    has_t = not (isinstance(T, int) and T > NT - 1)
                    for c in range(NG):
                        if has_t:
                            transposes(T, u, c)
                            if c >= LAG:
                                product(T, u, c - LAG)
                        if c in PLAN:
                            back, part = PLAN[c]
                            if not isinstance(T, int) or 0 <= T - back < NT:
                                gru(T - back, part)
                    if has_t:
                        for c in range(NG - LAG, NG):
                            product(T, u, c)

                slots(pe, slot, 0, NT + 1)

        GS = WH[:, :, :].rearrange("p t f -> p (t f)")[:, 0:NT * F].bitcast(f16).rearrange(
            "p (t f) -> p t f", f=2 * F)
        PH = [PT[b][:, 0:GC // 2].bitcast(f16) for b in range(NB)]
        low = gs[:, 0:F]
        xin = [rz[:, 0:F], rz[:, F:2 * F]]
        ot = [gs[:, F:2 * F], gs[:, 2 * F:3 * F]]
        unequal = sb("unequal", [P, NG])
        odd = sb("odd", [P, NG])
        differs = [sb(f"differs{b}", [P, GC], f16) for b in range(2)]
        ends = sb("ends", [P, 2])
        bad = sb("bad", [P, 2])
        onecol = sb("onecol", [P, 1])
        verdict = sb("verdict", [1, 1])
        redo = sb("redo", [1, 1], mybir.dt.int32)
        k_hi, k_v = sem("k_hi"), sem("k_v")
        with nc.Block() as block:
            @block.scalar
            def _(act):
                nc.scalar.activation(GS[:, :, 0:F], H[:, :, :], ACT.Copy, scale=GSCALE).then_inc(k_hi, 1)

            @block.gpsimd
            def _(pool):
                nc.gpsimd.memset(odd[:, :], 0.0).then_inc(k_v, 1)
                nc.gpsimd.memset(onecol[:, :], 1.0).then_inc(k_v, 1)

            @block.vector
            def _(dve):
                nc.vector.tensor_reduce(ends[:, 0:1], H[:, :, :].rearrange("p t f -> p (t f)"), AX.X,
                                        ALU.max).then_inc(k_v, 1)
                dve.wait_ge(k_hi, 1)
                nc.vector.scalar_tensor_tensor(GS[:, :, F:2 * F], H[:, :, :], GSCALE, GS[:, :, 0:F], ALU.mult,
                                               ALU.subtract).then_inc(k_v, 1)

        def pairs(eng, slot):
            for T in range(2):
                slot(T, T, 0)
            with eng.Fori(1, NT // 2) as k:
                for d in range(2):
                    slot(k * 2 + d, d, k)

        q_in, q_x = [sem(f"q_in{b}") for b in range(2)], [sem(f"q_x{b}") for b in range(2)]
        q_tr, q_pt, q_mm, q_o = sem("q_tr"), sem("q_pt"), sem("q_mm"), sem("q_o")
        q_ck = sem("q_ck")
        q_sum, q_lo = sem("q_sum"), sem("q_lo")
        q_out = [sem(f"q_out{b}") for b in range(2)]
        q_bad, q_all, q_say = sem("q_bad"), sem("q_all"), sem("q_say")
        SUMS = [OP, GP]
        with nc.Block() as block:
            @block.sync
            def _(sp):
                def slot(T, u, n):
                    wait(sp, q_tr, (T - 1) * NG)
                    sp.dma_start(Z[u][:, :], adj_t[T, :, :], max_dma_last_dim=8192).then_inc(q_in[u], 16)
                    wait(sp, q_o, T - 1)
                    sp.dma_start(xin[u], x1_t[T, :, :]).then_inc(q_x[u], 16)

                pairs(sp, slot)

            @block.tensor
            def _(pe):
                def slot(T, u, n):
                    def product(c):
                        pe.wait_ge(q_pt, T * NG + c + 1)
                        if c == 0:
                            wait(pe, q_o, T - 1)
                        for k in range(4):
                            j = 4 * c + k
                            ins = nc.tensor.matmul(SUMS[u][:, 0:2 * F], PH[c % NB][:, k * P:(k + 1) * P],
                                                   GS[:, j, :], start=(j == 0), stop=(j == NT - 1))
                        ins.then_inc(q_mm, 1)

                    for c in range(NG):
                        if c == 0:
                            pe.wait_ge(q_in[u], (n + 1) * 16)
                        wait(pe, q_ck, T * NG + c + 1 - NB)
                        for k in range(4):
                            j = 4 * c + k
                            ins = nc.tensor.transpose(TP[c % NB][:, k * P:(k + 1) * P], Z[u][:, j * P:(j + 1) * P],
                                                      ident[:, :])
                        ins.then_inc(q_tr, 1)
                        if c >= LAG:
                            product(c - LAG)
                    for c in range(NG - LAG, NG):
                        product(c)

                pairs(pe, slot)
                pe.wait_ge(q_bad, 6)
                nc.tensor.matmul(TG[0:1, 0:1], bad[:, 0:1], onecol[:, :], start=True, stop=True).then_inc(q_all, 1)

            @block.scalar
            def _(act):
                def slot(T, u, n):
                    for c in range(NG):
                        act.wait_ge(q_tr, T * NG + c + 1)
                        wait(act, q_mm, T * NG + c + 1 - NB)
                        wait(act, q_ck, T * NG + c + 1 - NB)
                        nc.scalar.activation(PH[c % NB], TP[c % NB][:, :], ACT.Copy).then_inc(q_pt, 1)

                pairs(act, slot)

            @block.vector
            def _(dve):
                def slot(T, u, n):
                    for c in range(NG):
                        dve.wait_ge(q_pt, T * NG + c + 1)
                        wait(dve, q_ck, T * NG + c - 1)
                        nc.vector.scalar_tensor_tensor(differs[c % 2][:, :], TP[c % NB][:, :], 0.0, PH[c % NB], ALU.add,
                                                       ALU.not_equal, accum_out=unequal[:, c:c + 1]).then_inc(q_ck, 1)
                        if c == 2:
                            finish(T - 1, 1 - u, n if u else n - 1)
                    dve.wait_ge(q_ck, (T + 1) * NG)
                    nc.vector.tensor_tensor(odd[:, :], odd[:, :], unequal[:, :], ALU.add).then_inc(q_sum, 1)
                    dve.wait_ge(q_sum, T + 1)

                def finish(T, u, n):
                    if isinstance(T, int) and T < 0:
                        return
                    dve.wait_ge(q_mm, (T + 1) * NG)
                    dve.wait_ge(q_x[u], (n + 1) * 16)
                    nc.vector.scalar_tensor_tensor(low, SUMS[u][:, F:2 * F], 1.0 / GSCALE, xin[u], ALU.mult,
                                                   ALU.add).then_inc(q_lo, 1)
                    dve.wait_ge(q_lo, T + 1)
                    if not (isinstance(T, int) and T < 2):
                        dve.wait_ge(q_out[u], n * 16)
                    nc.vector.scalar_tensor_tensor(ot[u], SUMS[u][:, 0:F], 1.0 / GSCALE, low, ALU.mult,
                                                   ALU.add).then_inc(q_o, 1)

                for T in range(3):
                    slot(T, T % 2, T // 2)
                with dve.Fori(1, NT // 2 - 1) as k:
                    for d in range(2):
                        slot(k * 2 + 1 + d, 1 - d, k + d)
                slot(NT - 1, 1, NT // 2 - 1)
                finish(NT - 1, 1, NT // 2 - 1)
                nc.vector.tensor_reduce(ends[:, 1:2], H[:, :, :].rearrange("p t f -> p (t f)"), AX.X,
                                        ALU.min).then_inc(q_bad, 1)
                dve.wait_ge(q_bad, 1)
                nc.vector.scalar_tensor_tensor(ends[:, 0:1], ends[:, 1:2], -1.0, ends[:, 0:1], ALU.mult,
                                               ALU.max).then_inc(q_bad, 1)
                nc.vector.tensor_reduce(bad[:, 1:2], odd[:, :], AX.X, ALU.add).then_inc(q_bad, 1)
                dve.wait_ge(q_bad, 3)
                nc.vector.tensor_scalar(bad[:, 0:1], ends[:, 0:1], GMOST, None, ALU.is_le).then_inc(q_bad, 1)
                dve.wait_ge(q_bad, 4)
                nc.vector.scalar_tensor_tensor(bad[:, 0:1], ends[:, 0:1], GLEAST, bad[:, 0:1], ALU.is_ge,
                                               ALU.mult).then_inc(q_bad, 1)
                dve.wait_ge(q_bad, 5)
                nc.vector.scalar_tensor_tensor(bad[:, 0:1], bad[:, 0:1], 0.5, bad[:, 1:2], ALU.is_lt,
                                               ALU.add).then_inc(q_bad, 1)
                dve.wait_ge(q_all, 1)
                nc.vector.tensor_scalar(verdict[:, :], TG[0:1, 0:1], 0.0, None, ALU.not_equal).then_inc(q_say, 1)
                dve.wait_ge(q_say, 1)
                nc.vector.tensor_copy(redo[:, :], verdict[:, :]).then_inc(q_say, 1)

            @block.gpsimd
            def _(pool):
                def slot(T, u, n):
                    pool.wait_ge(q_o, T + 1)
                    pool.dma_start(out_t[T, :, :], ot[u]).then_inc(q_out[u], 16)

                pairs(pool, slot)
                for b in range(2):
                    pool.wait_ge(q_out[b], NT // 2 * 16)

        l_in, l_x = [sem(f"l_in{b}") for b in range(2)], [sem(f"l_x{b}") for b in range(2)]
        l_tr, l_pt, l_mm, l_o = sem("l_tr"), sem("l_pt"), sem("l_mm"), sem("l_o")
        l_out = [sem(f"l_out{b}") for b in range(2)]
        OB = [OP, GP]
        needed = nc.values_load(redo[0:1, 0:1], min_val=0, max_val=1)
        with nc.If(needed != 0):
            with nc.Block() as block:
                @block.sync
                def _(sp):
                    def slot(T, u, n):
                        wait(sp, l_tr, (T - 1) * NG)
                        sp.dma_start(Z[u][:, :], adj_t[T, :, :], max_dma_last_dim=8192).then_inc(l_in[u], 16)
                        wait(sp, l_o, T - 1)
                        sp.dma_start(xin[u], x1_t[T, :, :]).then_inc(l_x[u], 16)

                    pairs(sp, slot)

                @block.tensor
                def _(pe):
                    def slot(T, u, n):
                        def product(c):
                            pe.wait_ge(l_pt, T * NG + c + 1)
                            if c == 0:
                                wait(pe, l_o, T - 1)
                            for k in range(4):
                                j = 4 * c + k
                                ins = nc.tensor.matmul(OB[u][:, 0:F], PT[c % NB][:, k * P:(k + 1) * P], H[:, j, :],
                                                       start=(j == 0), stop=(j == NT - 1))
                            ins.then_inc(l_mm, 1)

                        for c in range(NG):
                            if c == 0:
                                pe.wait_ge(l_in[u], (n + 1) * 16)
                            wait(pe, l_pt, T * NG + c + 1 - NB)
                            for k in range(4):
                                j = 4 * c + k
                                ins = nc.tensor.transpose(TP[c % NB][:, k * P:(k + 1) * P], Z[u][:, j * P:(j + 1) * P],
                                                          ident[:, :])
                            ins.then_inc(l_tr, 1)
                            if c >= LAG:
                                product(c - LAG)
                        for c in range(NG - LAG, NG):
                            product(c)

                    pairs(pe, slot)

                @block.scalar
                def _(act):
                    def slot(T, u, n):
                        for c in range(NG):
                            act.wait_ge(l_tr, T * NG + c + 1)
                            wait(act, l_mm, T * NG + c + 1 - NB)
                            nc.scalar.activation(PT[c % NB][:, :], TP[c % NB][:, :], ACT.Copy).then_inc(l_pt, 1)

                    pairs(act, slot)

                @block.vector
                def _(dve):
                    def slot(T, u, n):
                        dve.wait_ge(l_mm, (T + 1) * NG)
                        dve.wait_ge(l_x[u], (n + 1) * 16)
                        wait(dve, l_out[u], n * 16)
                        nc.vector.tensor_tensor(ot[u], OB[u][:, 0:F], xin[u], ALU.add).then_inc(l_o, 1)

                    pairs(dve, slot)

                @block.gpsimd
                def _(pool):
                    def slot(T, u, n):
                        pool.wait_ge(l_o, T + 1)
                        pool.dma_start(out_t[T, :, :], ot[u]).then_inc(l_out[u], 16)

                    pairs(pool, slot)
                    for b in range(2):
                        pool.wait_ge(l_out[b], NT // 2 * 16)


_INS = ['x', 'adj', 'L0_gnn_W', 'L0_gnn_a', 'L0_gnn_w_ih', 'L0_gnn_w_hh', 'L0_gnn_b_ih', 'L0_gnn_b_hh',
        'L1_gnn_W', 'L1_gnn_b']
_OUTS = [((8192, 128), 'float32')]


def kernel(**inputs):
    import numpy as _np
    import concourse.bacc as _bacc
    from concourse import mybir as _mybir
    from concourse.bass_utils import run_bass_kernel_spmd as _run

    nc = _bacc.Bacc("TRN2", target_bir_lowering=False, num_devices=1)
    arrays, args = {}, []
    for name in _INS:
        arr = _np.ascontiguousarray(inputs[name])
        arrays[f"in_{name}_dram"] = arr
        args.append(nc.dram_tensor(f"in_{name}_dram", arr.shape, _mybir.dt.from_np(arr.dtype),
                                   kind="ExternalInput").ap())
    for i, (shape, dtype) in enumerate(_OUTS):
        dt = _mybir.dt.from_np(_np.dtype(dtype))
        args.append(nc.dram_tensor(f"out_{i}_dram", shape, dt, kind="ExternalOutput").ap())
    graph_layers(nc, *args)
    r = _run(nc, [arrays], core_ids=[0])
    return r.results[0]["out_0_dram"]
```
